# Optimizing a Trainium2 kernel written in Bass

```python
import numpy as np
import jax
import jax.numpy as jnp

def _softmax(x, axis=-1):
    return jax.nn.softmax(x, axis=axis)

def _gelu(x):
    return jax.nn.gelu(x, approximate=True)

def _silu(x):
    return jax.nn.silu(x)

def _sigmoid(x):
    return jax.nn.sigmoid(x)

def _layernorm(x, axis=-1, eps=1e-05):
    m = jnp.mean(x, axis=axis, keepdims=True)
    v = jnp.var(x, axis=axis, keepdims=True)
    return (x - m) / jnp.sqrt(v + eps)

def _scatter_add(tgt, idx, src, axis=0):
    return tgt.at[idx].add(src)

def _segment_sum(src, seg, n):
    return jax.ops.segment_sum(src, seg, n)
kernel_name = 'mk_sandwich_d1_jaxref_r4_c457a6'

def setup_inputs(seed: int=0):
    np.random.seed(seed)
    _w = jnp.asarray

    def _L0_attn_setup():
        import jax, jax.numpy as jnp
        import numpy as np
        B, T, C, H = (2, 512, 256, 16)
        R = 32
        LORA_SCALE = 0.5
        HD = C // H

        def lora_linear(x, w, b, la, lb):
            return x @ w.T + b + LORA_SCALE * (x @ la.T @ lb.T)
        key = jax.random.key(seed)
        ks = jax.random.split(key, 8)
        std = 0.02
        return {'x': jax.random.normal(ks[0], (B, T, C), jnp.float32), 'w_attn': jax.random.normal(ks[1], (3 * C, C), jnp.float32) * std, 'b_attn': jnp.zeros((3 * C,), jnp.float32), 'la_attn': jax.random.normal(ks[2], (R, C), jnp.float32) * std, 'lb_attn': jax.random.normal(ks[3], (3 * C, R), jnp.float32) * std, 'w_proj': jax.random.normal(ks[4], (C, C), jnp.float32) * std, 'b_proj': jnp.zeros((C,), jnp.float32), 'la_proj': jax.random.normal(ks[5], (R, C), jnp.float32) * std, 'lb_proj': jax.random.normal(ks[6], (C, R), jnp.float32) * std}
    _L0_attn_in = _L0_attn_setup()

    def _L0_ffn_setup():
        import jax, jax.numpy as jnp
        import numpy as np
        GROUP = 16
        EPS = 1e-05

        def _dequant(q, scale):
            w = q.astype(jnp.float32) / 7.5 - 1.0
            return w * jnp.repeat(scale, GROUP, axis=1)

        def _qlora_linear(x, q, scale, bias, la, lb):
            w = _dequant(q, scale)
            base = jnp.einsum('btd,od->bto', x, w) + bias
            lora = jnp.einsum('btr,or->bto', jnp.einsum('btd,rd->btr', x, la), lb)
            return base + lora

        def _layernorm(x, g, b):
            mu = jnp.mean(x, axis=-1, keepdims=True)
            var = jnp.mean(jnp.square(x - mu), axis=-1, keepdims=True)
            return (x - mu) * jax.lax.rsqrt(var + EPS) * g + b
        key = jax.random.key(seed)
        ks = jax.random.split(key, 6)
        D, R, B, T = (256, 32, 8, 1024)
        x = jax.random.normal(ks[0], (B, T, D), dtype=jnp.float32)
        qweights = jax.random.randint(ks[1], (6, D, D), 0, 16, dtype=jnp.int32)
        scales = jax.random.uniform(ks[2], (6, D, D // GROUP), dtype=jnp.float32)
        biases = jax.random.normal(ks[3], (6, D), dtype=jnp.float32) * 0.02
        lora_a = jax.random.normal(ks[4], (6, R, D), dtype=jnp.float32) * 0.02
        lora_b = jax.random.normal(ks[5], (6, D, R), dtype=jnp.float32) * 0.02
        ln_gamma = jnp.ones((3, D), dtype=jnp.float32)
        ln_beta = jnp.zeros((3, D), dtype=jnp.float32)
        return {'x': x, 'qweights': qweights, 'scales': scales, 'biases': biases, 'lora_a': lora_a, 'lora_b': lora_b, 'ln_gamma': ln_gamma, 'ln_beta': ln_beta}
    _L0_ffn_in = _L0_ffn_setup()
    _d = {'L0_attn_x': _L0_attn_in['x'], 'L0_attn_w_attn': _L0_attn_in['w_attn'], 'L0_attn_b_attn': _L0_attn_in['b_attn'], 'L0_attn_la_attn': _L0_attn_in['la_attn'], 'L0_attn_lb_attn': _L0_attn_in['lb_attn'], 'L0_attn_w_proj': _L0_attn_in['w_proj'], 'L0_attn_b_proj': _L0_attn_in['b_proj'], 'L0_attn_la_proj': _L0_attn_in['la_proj'], 'L0_attn_lb_proj': _L0_attn_in['lb_proj'], 'L0_ffn_qweights': _L0_ffn_in['qweights'], 'L0_ffn_scales': _L0_ffn_in['scales'], 'L0_ffn_biases': _L0_ffn_in['biases'], 'L0_ffn_lora_a': _L0_ffn_in['lora_a'], 'L0_ffn_lora_b': _L0_ffn_in['lora_b'], 'L0_ffn_ln_gamma': _L0_ffn_in['ln_gamma'], 'L0_ffn_ln_beta': _L0_ffn_in['ln_beta']}
    _x0 = _d['L0_attn_x']
    _d['L0_attn_x'] = jax.random.normal(jax.random.fold_in(jax.random.key(seed), 1), (1, 4096, 256), dtype=_x0.dtype)
    del _x0
    return _d

def reference(L0_attn_x, L0_attn_w_attn, L0_attn_b_attn, L0_attn_la_attn, L0_attn_lb_attn, L0_attn_w_proj, L0_attn_b_proj, L0_attn_la_proj, L0_attn_lb_proj, L0_ffn_qweights, L0_ffn_scales, L0_ffn_biases, L0_ffn_lora_a, L0_ffn_lora_b, L0_ffn_ln_gamma, L0_ffn_ln_beta):

    def _L0_attn_ref(x, w_attn, b_attn, la_attn, lb_attn, w_proj, b_proj, la_proj, lb_proj):
        import jax, jax.numpy as jnp
        import numpy as np
        B, T, C, H = (2, 512, 256, 16)
        R = 32
        LORA_SCALE = 0.5
        HD = C // H

        def lora_linear(x, w, b, la, lb):
            return x @ w.T + b + LORA_SCALE * (x @ la.T @ lb.T)
        Bsz, Tlen, Cdim = x.shape
        qkv = lora_linear(x, w_attn, b_attn, la_attn, lb_attn)
        q, k, v = jnp.split(qkv, 3, axis=2)
        rs = lambda t: t.reshape(Bsz, Tlen, H, HD).transpose(0, 2, 1, 3)
        q, k, v = (rs(q), rs(k), rs(v))
        att = jnp.einsum('bhqd,bhkd->bhqk', q, k) * (1.0 / np.sqrt(HD))
        causal = jnp.tril(jnp.ones((Tlen, Tlen), dtype=bool))
        att = jnp.where(causal[None, None], att, -jnp.inf)
        att = jax.nn.softmax(att, axis=-1)
        y = jnp.einsum('bhqk,bhkd->bhqd', att, v)
        y = y.transpose(0, 2, 1, 3).reshape(Bsz, Tlen, Cdim)
        return lora_linear(y, w_proj, b_proj, la_proj, lb_proj)

    def _L0_ffn_ref(x, qweights, scales, biases, lora_a, lora_b, ln_gamma, ln_beta):
        import jax, jax.numpy as jnp
        import numpy as np
        GROUP = 16
        EPS = 1e-05

        def _dequant(q, scale):
            w = q.astype(jnp.float32) / 7.5 - 1.0
            return w * jnp.repeat(scale, GROUP, axis=1)

        def _qlora_linear(x, q, scale, bias, la, lb):
            w = _dequant(q, scale)
            base = jnp.einsum('btd,od->bto', x, w) + bias
            lora = jnp.einsum('btr,or->bto', jnp.einsum('btd,rd->btr', x, la), lb)
            return base + lora

        def _layernorm(x, g, b):
            mu = jnp.mean(x, axis=-1, keepdims=True)
            var = jnp.mean(jnp.square(x - mu), axis=-1, keepdims=True)
            return (x - mu) * jax.lax.rsqrt(var + EPS) * g + b
        h = x
        for blk in range(3):
            i0, i1 = (2 * blk, 2 * blk + 1)
            y = _qlora_linear(h, qweights[i0], scales[i0], biases[i0], lora_a[i0], lora_b[i0])
            y = _layernorm(y, ln_gamma[blk], ln_beta[blk])
            y = jax.nn.gelu(y, approximate=False)
            y = _qlora_linear(y, qweights[i1], scales[i1], biases[i1], lora_a[i1], lora_b[i1])
            h = y + h
        return h
    x = L0_attn_x
    x = x + _layernorm(_L0_attn_ref(_layernorm(x, axis=-1), L0_attn_w_attn, L0_attn_b_attn, L0_attn_la_attn, L0_attn_lb_attn, L0_attn_w_proj, L0_attn_b_proj, L0_attn_la_proj, L0_attn_lb_proj), axis=-1)
    x = x + _layernorm(_L0_ffn_ref(_layernorm(x, axis=-1), L0_ffn_qweights, L0_ffn_scales, L0_ffn_biases, L0_ffn_lora_a, L0_ffn_lora_b, L0_ffn_ln_gamma, L0_ffn_ln_beta), axis=-1)
    return x

_drawn_inputs = setup_inputs


def setup_inputs(seed=0):
    import zlib

    import numpy as np

    out = dict(_drawn_inputs(seed))
    spreads = {'L0_attn_b_attn': (0.0, 0.1),
     'L0_attn_b_proj': (0.0, 0.1),
     'L0_ffn_ln_gamma': (1.0, 0.2),
     'L0_ffn_ln_beta': (0.0, 0.1)}
    factors = {'L0_attn_la_attn': 8.0,
     'L0_attn_lb_attn': 8.0,
     'L0_attn_la_proj': 5.097,
     'L0_attn_lb_proj': 4.716,
     'L0_ffn_biases': 8.0,
     'L0_ffn_lora_a': 7.484,
     'L0_ffn_lora_b': 7.568}
    for name, (base, spread) in spreads.items():
        noise = np.random.default_rng([zlib.crc32(name.encode()), seed]).standard_normal(out[name].shape)
        drawn = base * np.exp(spread * noise) if base else spread * noise
        out[name] = jnp.asarray(drawn.astype(out[name].dtype))
    for name, factor in factors.items():
        out[name] = (out[name] * factor).astype(out[name].dtype)
    return out
```

```python
from contextlib import ExitStack

import concourse.bass as bass
from concourse import mybir

F32 = mybir.dt.float32
BF16 = mybir.dt.bfloat16
I32 = mybir.dt.int32
ALU = mybir.AluOpType
ACT = mybir.ActivationFunctionType
AX = mybir.AxisListType

P = 128
T, C, H = 4096, 256, 16
D = C // H
R = 32
NC = C // P
TT = 512
NB = TT // P
NT = T // TT
HG = 4
NG = H // HG
STRIP = 32
PARTS = 3
Q_PART = (0, 1, 2, 0, 1, 0)
K_PART = (0, 0, 0, 1, 1, 2)
SHIFT0 = D * len(Q_PART)
ROWS = SHIFT0 + PARTS
SCALE = D ** -0.5
EPS = 1e-5
GROUP = 16
BLK = 3
SAFE_SCORE = 40.0
NEG = -1.0e30
RSQRT_SEED = float(0x5F3759DF)
NEWTON = 3
RS_OPS = 4 * NEWTON + 3


def bcast(ap, n):
    return ap.unsqueeze(2).to_broadcast([ap.shape[0], ap.shape[1], n])


def hold(eng, sem, value, held):
    eng.wait_ge(sem, value)
    if not isinstance(value, int):
        eng.sem_inc(held, 1)


def pool_rsqrt(pool, nc, held, chain, base, mv, tmp, y, nmr):
    n = 0

    def step(ins):
        nonlocal n
        n += 1
        ins.then_inc(chain, 1)
        hold(pool, chain, base + n, held)

    hv, t = tmp[:, 2, :], tmp[:, 0, :]
    step(nc.gpsimd.tensor_scalar(hv, tmp[:, 1, :], -0.5, None, ALU.mult))
    for _ in range(NEWTON):
        step(nc.gpsimd.tensor_tensor(t, y, y, ALU.mult))
        step(nc.gpsimd.tensor_tensor(t, t, hv, ALU.mult))
        step(nc.gpsimd.tensor_scalar(t, t, 1.5, None, ALU.add))
        step(nc.gpsimd.tensor_tensor(y, y, t, ALU.mult))
    step(nc.gpsimd.tensor_tensor(t, mv[:, :, 0], y, ALU.mult))
    n += 1
    assert n == RS_OPS
    return nc.gpsimd.tensor_scalar(nmr, t, -1.0, None, ALU.mult)


def dve_stats(dve, nc, held, chain, base, src, st, mv, tmp, y):
    for b in range(NB):
        last = nc.vector.bn_stats(st[:, b, :], src[:, b, :])
    last.then_inc(chain, 1)
    hold(dve, chain, base + 1, held)
    for b in range(NB):
        last = nc.vector.bn_aggr(mv[:, b, :], st[:, b, :])
    last.then_inc(chain, 1)
    dve.wait_ge(chain, base + 2)
    nc.vector.tensor_scalar(tmp[:, 1, :], mv[:, :, 1], EPS, None, ALU.add).then_inc(chain, 1)
    dve.wait_ge(chain, base + 3)
    return nc.vector.tensor_scalar(y.bitcast(I32), tmp[:, 1, :].bitcast(I32), -0.5, RSQRT_SEED, ALU.mult, ALU.add)


def prepare_weights(nc, g, d):
    with ExitStack() as ctx:
        sb = lambda n, s, t: ctx.enter_context(nc.sbuf_tensor(n, s, t))
        sem = lambda n: ctx.enter_context(nc.semaphore(n))
        NA, NF = 3 * C // P, 2 * BLK * C // P
        NO = NA + NC + NF
        w_nat = sb("w_nat", [P, NO, C], F32)
        lb_nat = sb("lb_nat", [P, NO, R], F32)
        la = sb("la", [R, 2 + 2 * BLK, C], F32)
        lbT = sb("lbT", [R, NO * P], F32)
        q_int = sb("q_int", [P, NF, C], I32)
        scl = sb("scl", [P, NF, C // GROUP], F32)
        no_shift = sb("no_shift", [P, PARTS * H * T // P], BF16)
        shift_zero, shift_stored, ones_ok = sem("shift_zero"), sem("shift_stored"), sem("ones_ok")
        lbT_ps = ctx.enter_context(nc.psum_tensor("lbT_ps", [P, NO * P], F32))
        wT_ps = ctx.enter_context(nc.psum_tensor("wT_ps", [P, 3, 2 * C], F32))
        small_in, w_in, q_in, la_in = sem("small_in"), sem("w_in"), sem("q_in"), sem("la_in")
        zeroed, ident_ok, dequant, transposed, lbT_ok = (sem(n) for n in ("zeroed", "ident_ok", "dequant", "transposed", "lbT_ok"))
        summed, wT_act, wT_dve = sem("summed"), sem("wT_act"), sem("wT_dve")
        mats = [(2 * m, 0, g["wqkvT"][:, :, m * C:(m + 1) * C]) for m in range(3)]
        mats += [(NA, 1, g["wpT"][:, :, :])]
        mats += [(NA + NC + 2 * m, 2 + m, g["wfT"][:, m, :, :]) for m in range(2 * BLK)]
        with nc.Block() as block:

            @block.sync
            def _(sp):
                sp.dma_start(lb_nat[:, 0:NA, :], d["lb_attn"].rearrange("(m p) r -> p m r", p=P)).then_inc(la_in, 16)
                sp.dma_start(lb_nat[:, NA:NA + NC, :], d["lb_proj"].rearrange("(m p) r -> p m r", p=P)).then_inc(la_in, 16)
                sp.dma_start(lb_nat[:, NA + NC:, :], d["lora_b"].rearrange("k (m p) r -> p (k m) r", p=P)).then_inc(la_in, 16)
                sp.dma_start(w_nat[:, 0:NA, :], d["w_attn"].rearrange("(m p) i -> p m i", p=P)).then_inc(w_in, 16)
                sp.dma_start(w_nat[:, NA:NA + NC, :], d["w_proj"].rearrange("(m p) i -> p m i", p=P)).then_inc(w_in, 16)
                sp.dma_start(la[:, 0, :], d["la_attn"]).then_inc(w_in, 16)
                sp.dma_start(la[:, 1, :], d["la_proj"]).then_inc(w_in, 16)
                sp.dma_start(la[:, 2:, :], d["lora_a"].rearrange("k r i -> r k i")).then_inc(w_in, 16)
                for m in range(2 * C // P):
                    sp.dma_start(g["bqk"][:, m:m + 1], d["b_attn"][m * P:(m + 1) * P].rearrange("(p o) -> p o", o=1)).then_inc(small_in, 16)
                for m in range(BLK * NC):
                    at = slice((m % NC) * P, (m % NC + 1) * P)
                    sp.dma_start(g["gamma"][:, m:m + 1], d["ln_gamma"][m // NC, at].rearrange("(p o) -> p o", o=1)).then_inc(small_in, 16)
                    sp.dma_start(g["beta"][:, m:m + 1], d["ln_beta"][m // NC, at].rearrange("(p o) -> p o", o=1)).then_inc(small_in, 16)
                sp.wait_ge(shift_zero, 1)
                sp.dma_start(d["shift"].rearrange("s h t -> (s h t)").rearrange("(p n) -> p n", p=P), no_shift[:, :]).then_inc(shift_stored, 16)
                sp.wait_ge(shift_stored, 16)
                sp.wait_ge(small_in, 16 * (2 * C // P + 2 * BLK * NC + 3))

            @block.scalar
            def _(act):
                act.dma_start(q_int[:, :, :], d["qweights"].rearrange("k (m p) i -> p (k m) i", p=P)).then_inc(q_in, 16)
                act.dma_start(scl[:, :, :], d["scales"].rearrange("k (m p) g -> p (k m) g", p=P)).then_inc(q_in, 16)
                act.dma_start(g["bv"][:, :], d["b_attn"][2 * C:3 * C].rearrange("(o c) -> o c", o=1).to_broadcast([P, C])).then_inc(small_in, 16)
                act.dma_start(g["bproj"][:, :], d["b_proj"].rearrange("(o c) -> o c", o=1).to_broadcast([P, C])).then_inc(small_in, 16)
                act.dma_start(g["bffn"][:, :], d["biases"].rearrange("(o k) c -> o (k c)", o=1).to_broadcast([P, 2 * BLK * C])).then_inc(small_in, 16)
                act.wait_ge(transposed, 1)
                nc.scalar.activation(lbT[:, 0:(NA + NC) * P], lbT_ps[0:R, 0:(NA + NC) * P], ACT.Copy, scale=0.5)
                nc.scalar.activation(lbT[:, (NA + NC) * P:], lbT_ps[0:R, (NA + NC) * P:], ACT.Copy).then_inc(lbT_ok, 1)
                for n in range(0, 2 * len(mats), 2):
                    dst = mats[n // 2][2]
                    act.wait_ge(summed, n + 1)
                    nc.scalar.copy(dst[:, 0, :], wT_ps[:, n % 3, 0:C]).then_inc(wT_act, 1)

            @block.gpsimd
            def _(pool):
                nc.gpsimd.memset(no_shift[:, :], 0.0).then_inc(shift_zero, 1)
                nc.gpsimd.memset(g["ident"][:, :], 0.0).then_inc(zeroed, 1)
                pool.wait_ge(zeroed, 1)
                nc.gpsimd.affine_select(out=g["ident"][:, :], in_=g["ident"][:, :], compare_op=ALU.not_equal, fill=1.0,
                                        base=0, pattern=[[-1, P]], channel_multiplier=1).then_inc(ident_ok, 1)
                nc.gpsimd.memset(g["vg"][:, :, :, D:STRIP], 1.0).then_inc(ones_ok, 1)
                pool.wait_ge(ones_ok, 1)
                nc.gpsimd.memset(g["k_op"][SHIFT0:ROWS, :, :], 1.0).then_inc(ones_ok, 1)
                pool.wait_ge(ones_ok, 2)

            @block.vector
            def _(dve):
                wf = w_nat[:, NA + NC:, :]
                dve.wait_ge(q_in, 32)
                nc.vector.tensor_scalar(wf, q_int[:, :, :], 1.0 / 7.5, -1.0, ALU.mult, ALU.add).then_inc(dequant, 1)
                dve.wait_ge(dequant, 1)
                for m in range(NF):
                    last = nc.vector.tensor_tensor(wf[:, m, :].rearrange("p (g e) -> p g e", e=GROUP),
                                                   wf[:, m, :].rearrange("p (g e) -> p g e", e=GROUP),
                                                   bcast(scl[:, m, :], GROUP), ALU.mult)
                last.then_inc(dequant, 1)
                for n in range(1, 2 * len(mats), 2):
                    dst = mats[n // 2][2]
                    dve.wait_ge(summed, n + 1)
                    nc.vector.tensor_copy(dst[:, 1, :], wT_ps[:, n % 3, 0:C]).then_inc(wT_dve, 1)

            @block.tensor
            def _(pe):
                pe.wait_ge(ident_ok, 1)
                pe.wait_ge(la_in, 48)
                for m in range(NO):
                    last = nc.tensor.transpose(lbT_ps[0:R, m * P:(m + 1) * P], lb_nat[:, m, :], g["ident"][:, :])
                last.then_inc(transposed, 1)
                pe.wait_ge(lbT_ok, 1)
                pe.wait_ge(w_in, 80)
                for n in range(2 * len(mats)):
                    o0, a, _ = mats[n // 2]
                    c = n % 2
                    if o0 == NA + NC:
                        pe.wait_ge(dequant, 2)
                    if n >= 3 and (n - 3) % 2 == 0:
                        pe.wait_ge(wT_act, (n - 3) // 2 + 1)
                    elif n >= 3:
                        pe.wait_ge(wT_dve, (n - 3) // 2 + 1)
                    for o in range(2):
                        ps = wT_ps[:, n % 3, o * P:(o + 1) * P]
                        nc.tensor.matmul(ps, w_nat[:, o0 + o, c * P:(c + 1) * P], g["ident"][:, :], start=True, stop=False)
                        last = nc.tensor.matmul(ps, la[:, a, c * P:(c + 1) * P], lbT[:, (o0 + o) * P:(o0 + o + 1) * P],
                                                start=False, stop=True)
                    last.then_inc(summed, 1)


def project(nc, g, d):
    with ExitStack() as ctx:
        sb = lambda n, s, t: ctx.enter_context(nc.sbuf_tensor(n, s, t))
        ps = lambda n, s: ctx.enter_context(nc.psum_tensor(n, s, F32))
        sem = lambda n: ctx.enter_context(nc.semaphore(n))
        x_in = sb("x_in", [P, 2, NB, C], F32)
        xn = sb("xn", [P, 2, NB, C], F32)
        xnT = sb("xnT", [P, 2, NC, TT], F32)
        qf = sb("qf", [P, 2, TT], F32)
        res = sb("res", [P, 2, TT], F32)
        parts = sb("parts", [P, 4, PARTS, TT], BF16)
        st = sb("stA", [P, 2, NB, 6], F32)
        mv = sb("mvA", [P, 2, NB, 2], F32)
        tmp = sb("tmpA", [P, 2, 3, NB], F32)
        rstd = sb("rstdA", [P, 2, NB], F32)
        nmr = sb("nmrA", [P, 2, NB], F32)
        sq = sb("sq", [P, 4, TT], BF16)
        heads_of = sb("heads_of", [P, STRIP], BF16)
        norms = sb("norms", [P, NT], F32)
        norm_max = sb("norm_max", [P, 1], F32)
        bound = sb("bound", [1, P // 2 + 2], F32)
        psT = ps("psT", [P, NC, TT])
        psQ = ps("psQ", [P, 4, TT])
        psV = ps("psV", [P, NB, C])
        x_loaded = [sem(f"x_loaded{u}") for u in range(2)]
        stored = [sem(f"stored{m}") for m in range(4)]
        dve_chain, pool_chain = sem("dve_chainA"), sem("pool_chainA")
        stats_ok, rstd_ok, norm_ok, turned, xT_ok = (sem(n) for n in ("stats_ok", "rstd_ok", "norm_ok", "turned", "xT_ok"))
        qk_ok, full_ok, res_ok, split_ok, v_ok, v_out = (sem(n) for n in ("qk_ok", "full_ok", "res_ok", "split_ok", "v_ok", "v_out"))
        x_tiles = d["x"][0].rearrange("(t b p) c -> t p b c", b=NB, p=P)
        held = sem("heldA")
        sel0, sel1, sel_ok, sq_ok, norm_done, norm_read, bound_chain = (
            sem(n) for n in ("sel0", "sel1", "sel_ok", "sq_ok", "norm_done", "norm_read", "bound_chain"))
        SLOTS, BANKS = 2, 4

        def rounds(eng, tile, first=None):
            if first:
                first()
            with eng.Fori(0, NT // 2 - 1) as i:
                for u in range(2):
                    tile(i, u, False)
            for u in range(2):
                tile(NT // 2 - 1, u, u == 1)

        with nc.Block() as block:

            @block.sync
            def _(sp):
                for u in range(2):
                    sp.dma_start(x_in[:, u, :, :], x_tiles[u]).then_inc(x_loaded[u], 16)

                def tile(i, u, last):
                    n = i * 2 + u
                    if not isinstance(i, int):
                        hold(sp, norm_ok, n + 1, held)
                        sp.dma_start(x_in[:, u, :, :], x_tiles[n + 2]).then_inc(x_loaded[u], 16)
                    for m in range(4):
                        hold(sp, split_ok, n * 4 + m + 1 + SLOTS, held)
                        dst = d["qk_parts"][m // 2, :, (m % 2) * P:(m % 2 + 1) * P, bass.ds(n * TT, TT)]
                        sp.dma_start(dst.rearrange("s p t -> p s t"), parts[:, m, :, :]).then_inc(stored[m], 16)

                rounds(sp, tile)
                for m in range(4):
                    sp.wait_ge(stored[m], 16 * (1 + NT))

            @block.scalar
            def _(act):
                for m in range(4):
                    act.sem_inc(stored[m], 16)
                act.sem_inc(full_ok, BANKS)
                act.sem_inc(norm_done, 1)

                def normalise(n, u):
                    act.wait_ge(rstd_ok, n + 1)
                    for b in range(NB):
                        last = nc.scalar.activation(xn[:, u, b, :], x_in[:, u, b, :], ACT.Identity,
                                                    bias=nmr[:, u, b:b + 1], scale=rstd[:, u, b:b + 1])
                    last.then_inc(norm_ok, 1)

                def copy_turned(n, u):
                    act.wait_ge(turned, n + 1)
                    nc.scalar.copy(xnT[:, u, :, :], psT[:, :, :]).then_inc(xT_ok, 1)

                def first():
                    normalise(0, 0)
                    copy_turned(0, 0)

                def tile(i, u, last):
                    n = i * 2 + u
                    for m in range(4):
                        act.wait_ge(qk_ok, n * 4 + m + 1)
                        act.wait_ge(split_ok, n * 4 + m + 1)
                        act.wait_ge(stored[m], (n + 1) * 16)
                        nc.scalar.activation(qf[:, m % 2, :], psQ[:, m, :], ACT.Identity, bias=g["bqk"][:, m:m + 1])
                        if m == 0:
                            act.wait_ge(norm_done, n + 1)
                        nc.scalar.activation(sq[:, m, :], psQ[:, m, :], ACT.Square, bias=g["bqk"][:, m:m + 1]).then_inc(sq_ok, 1)
                        nc.scalar.activation(parts[:, m, 0, :], psQ[:, m, :], ACT.Identity,
                                             bias=g["bqk"][:, m:m + 1]).then_inc(full_ok, 1)
                        if m == 1 and not last:
                            normalise(n + 1, 1 - u)
                    if not last:
                        copy_turned(n + 1, 1 - u)

                rounds(act, tile, first)

            @block.gpsimd
            def _(pool):
                nc.gpsimd.memset(heads_of[:, :], 1.0).then_inc(sel0, 1)
                pool.wait_ge(sel0, 1)
                nc.gpsimd.affine_select(out=heads_of[:, :], in_=heads_of[:, :], compare_op=ALU.is_ge, fill=0.0,
                                        base=0, pattern=[[-D, STRIP]], channel_multiplier=1).then_inc(sel1, 1)
                pool.wait_ge(sel1, 1)
                nc.gpsimd.affine_select(out=heads_of[:, :], in_=heads_of[:, :], compare_op=ALU.is_ge, fill=0.0,
                                        base=D - 1, pattern=[[D, STRIP]], channel_multiplier=-1).then_inc(sel_ok, 1)

                def rsqrt(n, u):
                    hold(pool, stats_ok, n + 1, held)
                    pool_rsqrt(pool, nc, held, pool_chain, n * (RS_OPS - 1), mv[:, u], tmp[:, u], rstd[:, u],
                               nmr[:, u]).then_inc(rstd_ok, 1)

                def tile(i, u, last):
                    if not last:
                        rsqrt(i * 2 + u + 1, 1 - u)

                rounds(pool, tile, lambda: rsqrt(0, 0))

            @block.vector
            def _(dve):
                dve.sem_inc(split_ok, SLOTS)

                def stats(n, u, loads):
                    dve.wait_ge(x_loaded[u], loads * 16)
                    dve_stats(dve, nc, held, dve_chain, n * 3, x_in[:, u], st[:, u], mv[:, u], tmp[:, u],
                              rstd[:, u]).then_inc(stats_ok, 1)

                def tile(i, u, last):
                    n = i * 2 + u
                    if not last:
                        dve.wait_ge(norm_ok, n + 1)
                        stats(n + 1, 1 - u, i + 1 + u)
                    for m in range(4):
                        s = m % 2
                        dve.wait_ge(full_ok, n * 4 + m + 1 + BANKS)
                        nc.vector.tensor_tensor(res[:, s, :], qf[:, s, :], parts[:, m, 0, :], ALU.subtract).then_inc(res_ok, 1)
                        dve.wait_ge(res_ok, n * 8 + m * 2 + 1)
                        nc.vector.tensor_copy(parts[:, m, 1, :], res[:, s, :]).then_inc(res_ok, 1)
                        dve.wait_ge(res_ok, n * 8 + m * 2 + 2)
                        nc.vector.tensor_tensor(parts[:, m, 2, :], res[:, s, :], parts[:, m, 1, :], ALU.subtract).then_inc(split_ok, 1)
                    dve.wait_ge(v_ok, n + 1)
                    nc.vector.tensor_tensor(g["v_all"][:, bass.ds(n * NB, NB), :], psV[:, :, :],
                                            g["bv"][:, :].unsqueeze(1).to_broadcast([P, NB, C]), ALU.add).then_inc(v_out, 1)
                    dve.wait_ge(norm_done, n + 1 + 1)
                    nc.vector.reduce_max(norms[:, bass.ds(n, 1)], psQ[:, 3, :], AX.X).then_inc(norm_read, 1)

                rounds(dve, tile, lambda: stats(0, 0, 1))
                dve.wait_ge(norm_read, NT + 1)
                nc.vector.reduce_max(norm_max[:, :], norms[:, :], AX.X).then_inc(bound_chain, 1)
                dve.wait_ge(norm_done, NT + 2)
                nc.vector.tensor_copy(bound[:, 2:], psQ[0:1, 0, 0:P // 2]).then_inc(bound_chain, 1)
                dve.wait_ge(bound_chain, 2)
                nc.vector.tensor_tensor(bound[:, 2:], bound[:, 2:], psQ[0:1, 0, P // 2:P], ALU.mult).then_inc(bound_chain, 1)
                dve.wait_ge(bound_chain, 3)
                nc.vector.reduce_max(bound[:, 0:1], bound[:, 2:], AX.X).then_inc(bound_chain, 1)
                dve.wait_ge(bound_chain, 4)
                nc.vector.tensor_scalar(bound[:, 1:2], bound[:, 0:1], (SAFE_SCORE / SCALE) ** 2, None, ALU.is_le).then_inc(bound_chain, 1)
                dve.wait_ge(bound_chain, 5)
                nc.vector.tensor_scalar(g["need_max"][:, :], bound[:, 1:2], -1.0, 1.0, ALU.mult, ALU.add).then_inc(bound_chain, 1)

            @block.tensor
            def _(pe):
                pe.sem_inc(v_out, 1)
                pe.sem_inc(norm_read, 1)
                pe.wait_ge(sel_ok, 1)

                def turn(n, u):
                    pe.wait_ge(norm_ok, n + 1)
                    for c in range(NC):
                        for b in range(NB):
                            last = nc.tensor.transpose(psT[:, c, b * P:(b + 1) * P], xn[:, u, b, c * P:(c + 1) * P], g["ident"][:, :])
                    last.then_inc(turned, 1)

                def tile(i, u, last):
                    n = i * 2 + u
                    pe.wait_ge(xT_ok, n + 1)
                    for m in range(4):
                        pe.wait_ge(full_ok, n * 4 + m + 1)
                        if m == 3:
                            pe.wait_ge(norm_read, n + 1)
                        for c in range(NC):
                            last_mm = nc.tensor.matmul(psQ[:, m, :], g["wqkvT"][:, c, m * P:(m + 1) * P], xnT[:, u, c, :],
                                                       start=(c == 0), stop=(c == NC - 1))
                        last_mm.then_inc(qk_ok, 1)
                    if not last:
                        turn(n + 1, 1 - u)
                    pe.wait_ge(v_out, n + 1)
                    for b in range(NB):
                        for c in range(NC):
                            last_mm = nc.tensor.matmul(psV[:, b, :], xnT[:, u, c, b * P:(b + 1) * P], g["wqkvT"][:, c, 2 * C:3 * C],
                                                       start=(c == 0), stop=(c == NC - 1))
                    last_mm.then_inc(v_ok, 1)
                    pe.wait_ge(full_ok, n * 4 + 4 + BANKS)
                    for m in range(4):
                        last_mm = nc.tensor.matmul(psQ[m * STRIP:(m + 1) * STRIP, 3, :], heads_of[:, :], sq[:, m, :],
                                                   start=True, stop=True)
                    last_mm.then_inc(norm_done, 1)

                rounds(pe, tile, lambda: turn(0, 0))
                pe.wait_ge(bound_chain, 1)
                nc.tensor.matmul(psQ[0:1, 0, 0:P], norm_max[:, :], g["ident"][:, :], start=True, stop=True).then_inc(norm_done, 1)


def load_parts(eng, d, op, kinds, which, h0, tok, done):
    for r, part in enumerate(kinds):
        src = d["qk_parts"][which, part, bass.ds(h0 * D, HG * D), tok].rearrange("(a e) t -> e a t", e=D)
        eng.dma_start(op[r * D:(r + 1) * D, :, tok], src).then_inc(done, 16)


def guard(nc, g, d):
    QB = T // P
    KEYS = 4 * TT
    chunks = [(b, k) for b in range(QB) for k in range(0, (b + 1) * P, KEYS)]
    NCH = len(chunks)
    STEPS = HG * NCH + 1
    with ExitStack() as ctx:
        sb = lambda n, s, t: ctx.enter_context(nc.sbuf_tensor(n, s, t))
        sem = lambda n: ctx.enter_context(nc.semaphore(n))
        q_op, k_op = g["q_op"], g["k_op"]
        ident_b = sb("ident_b", [P, P], BF16)
        unseen = sb("unseen", [P, P], BF16)
        mx = sb("mx", [P, 2, HG * QB], F32)
        top = sb("top", [P, HG * QB], F32)
        neg = sb("neg", [P, P], F32)
        rest = sb("rest", [P, P], F32)
        sh = sb("sh", [P, PARTS, P], BF16)
        S = ctx.enter_context(nc.psum_tensor("SG", [P, 2, KEYS], F32))
        op_loaded, op_used, scored, reduced, tops_ok = (sem(n) for n in ("op_loadedG", "op_used", "scored", "reduced", "tops_ok"))
        z_ok, masks_ok, chain, sh_ok, sh_stored = (sem(n) for n in ("z_ok", "masks_ok", "chainG", "sh_ok", "sh_stored"))
        held = sem("heldG")
        shift_rows = d["shift"].rearrange("s (g a) (b q) -> g (a b) s q", a=HG, q=P)
        LOADS = len(Q_PART) + len(K_PART)
        with nc.Block() as block:

            @block.sync
            def _(sp):
                need = sp.value_load(g["need_max"][0:1, 0:1], min_val=0, max_val=1)
                with sp.If(need == 1):
                    sp.sem_inc(op_used, 1)
                    with sp.Fori(0, NG) as i:
                        hold(sp, op_used, i + 1, held)
                        load_parts(sp, d, q_op, Q_PART, 0, i * HG, slice(0, T), op_loaded)
                        load_parts(sp, d, k_op, K_PART, 1, i * HG, slice(0, T), op_loaded)

            @block.scalar
            def _(act):
                need = act.value_load(g["need_max"][0:1, 0:1], min_val=0, max_val=1)
                with act.If(need == 1):
                    act.sem_inc(sh_stored, 16)
                    with act.Fori(0, NG) as i:
                        act.wait_ge(sh_ok, i + 1)
                        act.dma_start(shift_rows[i], sh[:, :, :]).then_inc(sh_stored, 16)
                    act.wait_ge(sh_stored, 16 * (NG + 1))

            @block.gpsimd
            def _(pool):
                need = pool.value_load(g["need_max"][0:1, 0:1], min_val=0, max_val=1)
                with pool.If(need == 1):
                    nc.gpsimd.memset(ident_b[:, :], 0.0).then_inc(z_ok, 1)
                    nc.gpsimd.memset(unseen[:, :], 0.0).then_inc(z_ok, 1)
                    pool.wait_ge(z_ok, 2)
                    nc.gpsimd.affine_select(out=ident_b[:, :], in_=ident_b[:, :], compare_op=ALU.not_equal, fill=1.0,
                                            base=0, pattern=[[-1, P]], channel_multiplier=1).then_inc(masks_ok, 1)
                    nc.gpsimd.affine_select(out=unseen[:, :], in_=unseen[:, :], compare_op=ALU.is_ge, fill=NEG,
                                            base=0, pattern=[[-1, P]], channel_multiplier=1).then_inc(masks_ok, 1)

            @block.vector
            def _(dve):
                need = dve.value_load(g["need_max"][0:1, 0:1], min_val=0, max_val=1)
                with dve.If(need == 1):
                    dve.sem_inc(reduced, 2)
                    nc.vector.memset(mx[:, 1, :], 3.0 * NEG).then_inc(chain, 1)
                    dve.wait_ge(chain, 1)
                    with dve.Fori(0, NG) as i:
                        with dve.Fori(0, HG) as a:
                            for c, (b, k) in enumerate(chunks):
                                w = min(KEYS, (b + 1) * P - k)
                                dve.wait_ge(scored, i * STEPS + a * NCH + c + 1)
                                nc.vector.reduce_max(mx[:, k // KEYS, bass.ds(a * QB + b, 1)], S[:, c % 2, 0:w], AX.X).then_inc(reduced, 1)
                        dve.wait_ge(reduced, i * STEPS + HG * NCH + 2)
                        nc.vector.tensor_tensor(top[:, :], mx[:, 0, :], mx[:, 1, :], ALU.max).then_inc(tops_ok, 1)
                        dve.wait_ge(scored, i * STEPS + STEPS)
                        nc.vector.tensor_scalar(neg[:, :], S[:, 0, 0:P], -1.0, None, ALU.mult).then_inc(reduced, 1)
                        dve.wait_ge(reduced, i * STEPS + STEPS + 2)
                        dve.wait_ge(sh_stored, i * 16 + 16)
                        nc.vector.tensor_copy(sh[:, 0, :], neg[:, :]).then_inc(chain, 1)
                        dve.wait_ge(chain, i * 4 + 2)
                        nc.vector.tensor_tensor(rest[:, :], neg[:, :], sh[:, 0, :], ALU.subtract).then_inc(chain, 1)
                        dve.wait_ge(chain, i * 4 + 3)
                        nc.vector.tensor_copy(sh[:, 1, :], rest[:, :]).then_inc(chain, 1)
                        dve.wait_ge(chain, i * 4 + 4)
                        nc.vector.tensor_tensor(sh[:, 2, :], rest[:, :], sh[:, 1, :], ALU.subtract).then_inc(sh_ok, 1)
                        dve.sem_inc(chain, 1)

            @block.tensor
            def _(pe):
                need = pe.value_load(g["need_max"][0:1, 0:1], min_val=0, max_val=1)
                with pe.If(need == 1):
                    pe.wait_ge(masks_ok, 2)
                    with pe.Fori(0, NG) as i:
                        pe.wait_ge(op_loaded, i * (LOADS * 16) + LOADS * 16)
                        hold(pe, reduced, i * STEPS + 2, held)
                        with pe.Fori(0, HG) as a:
                            for c, (b, k) in enumerate(chunks):
                                pe.wait_ge(reduced, i * STEPS + a * NCH + c + 1)
                                end = (b + 1) * P
                                for k0 in range(k, min(k + KEYS, end), TT):
                                    w = min(TT, end - k0)
                                    diag = k0 + w == end
                                    last = nc.tensor.matmul(S[:, c % 2, k0 - k:k0 - k + w], q_op[0:SHIFT0, a, b * P:(b + 1) * P],
                                                            k_op[0:SHIFT0, a, k0:k0 + w], start=True, stop=not diag)
                                    if diag:
                                        last = nc.tensor.matmul(S[:, c % 2, end - P - k:end - k], ident_b[:, :], unseen[:, :],
                                                                start=False, stop=True)
                                last.then_inc(scored, 1)
                        pe.wait_ge(tops_ok, i + 1)
                        nc.tensor.transpose(S[:, 0, 0:P], top[:, :], g["ident"][:, :]).then_inc(scored, 1)
                        pe.sem_inc(op_used, 1)


def attend(nc, g, d):
    with ExitStack() as ctx:
        sb = lambda n, s, t: ctx.enter_context(nc.sbuf_tensor(n, s, t))
        sem = lambda n: ctx.enter_context(nc.semaphore(n))
        NS, NP = 3, 6
        q_op, k_op, vg = g["q_op"], g["k_op"], g["vg"]
        probs = sb("probs", [P, NP, 2, TT], F32)
        acc = sb("acc", [P, 2, TT], F32)
        S = ctx.enter_context(nc.psum_tensor("S", [P, NS, 2, TT], F32))
        O = ctx.enter_context(nc.psum_tensor("O", [P, 2, TT], F32))
        held = sem("heldB")
        op_loaded = [sem(f"op_loaded{s}") for s in range(NT)]
        acc_stored = [sem(f"acc_stored{s}") for s in range(2)]
        vg_ok, scored, exp_ok, cut_ok, pv_ok, acc_ok = (
            sem(n) for n in ("vg_ok", "scoredB", "exp_ok", "cut_ok", "pv_ok", "acc_ok"))
        LOADS = len(Q_PART) + len(K_PART) + 1

        blocks = []
        for o, j in enumerate(range(NT - 1, -1, -1)):
            blocks += [(o, j, j * NB + b, b * P) for b in range(NB)]
            blocks += [(o, j, s * NB + b, 0) for s in range(j - 1, -1, -1) for b in range(NB)]
        NBLK = len(blocks)
        NPAIR = 2 * NBLK
        DIAG = 2 * NB * NT
        LAG = 2
        assert NPAIR % NS == 0 and NPAIR % NP == 0 and NT % 2 == 0

        def last_of_tile(n):
            return n + 1 == NBLK or blocks[n + 1][0] != blocks[n][0]

        def tile_done(i, o):
            return i * NBLK + sum(x[0] <= o for x in blocks) + NP // 2

        with nc.Block() as block:

            @block.sync
            def _(sp):
                def load(i, s):
                    tok = slice(s * TT, (s + 1) * TT)
                    load_parts(sp, d, q_op, Q_PART, 0, i * HG, tok, op_loaded[s])
                    load_parts(sp, d, k_op, K_PART, 1, i * HG, tok, op_loaded[s])
                    sp.dma_start(q_op[SHIFT0:ROWS, :, tok], d["shift"][:, bass.ds(i * HG, HG), tok]).then_inc(op_loaded[s], 16)

                def store(i, o):
                    hold(sp, acc_ok, i * NT + o + 1 + 2, held)
                    sp.dma_start(d["acc"][i, NT - 1 - o], acc[:, o % 2, :]).then_inc(acc_stored[o % 2], 16)

                for o in range(NT):
                    load(0, NT - 1 - o)
                with sp.Fori(1, NG) as i:
                    for o in range(NT):
                        hold(sp, pv_ok, tile_done(i - 1, o), held)
                        load(i, NT - 1 - o)
                        store(i - 1, o)
                for o in range(NT):
                    store(NG - 1, o)
                for s in range(2):
                    sp.wait_ge(acc_stored[s], 16 * (1 + NG * NT // 2))

            @block.gpsimd
            def _(pool):
                def take_v(i, o):
                    s = NT - 1 - o
                    at = slice(s * NB, (s + 1) * NB)
                    nc.gpsimd.tensor_copy(vg[:, at, :, 0:D], g["v_all"][:, at, bass.ds(i * (HG * D), HG * D)]
                                          .rearrange("p b (a e) -> p b a e", e=D)).then_inc(vg_ok, 1)

                def cut(i):
                    n = 0
                    for b, (o, j, kb, q0) in enumerate(blocks):
                        if kb < j * NB:
                            continue
                        for pair in (2 * b, 2 * b + 1):
                            hold(pool, exp_ok, i * NPAIR + pair + 1 + NS, held)
                            tri = probs[:, pair % NP, :, 0:P]
                            nc.gpsimd.affine_select(out=tri, in_=tri, compare_op=ALU.is_ge, fill=0.0, base=0,
                                                    pattern=[[0, 2], [1, P]], channel_multiplier=-1).then_inc(cut_ok, 1)
                            n += 1
                    assert n == DIAG

                for o in range(NT):
                    take_v(0, o)
                with pool.Fori(0, NG - 1) as i:
                    cut(i)
                    for o in range(NT):
                        pool.wait_ge(pv_ok, tile_done(i, o))
                        take_v(i + 1, o)
                cut(NG - 1)

            @block.scalar
            def _(act):
                act.sem_inc(exp_ok, NS)
                with act.Fori(0, NG) as i:
                    for b, (o, j, kb, q0) in enumerate(blocks):
                        for pair in (2 * b, 2 * b + 1):
                            act.wait_ge(scored, i * NPAIR + pair + 1)
                            act.wait_ge(pv_ok, i * NBLK + b - NP // 2 + 1 + NP // 2)
                            nc.scalar.activation(probs[:, pair % NP, :, 0:TT - q0], S[:, pair % NS, :, 0:TT - q0], ACT.Exp,
                                                 scale=SCALE).then_inc(exp_ok, 1)

            @block.vector
            def _(dve):
                dve.sem_inc(acc_ok, 2)
                for s in range(2):
                    dve.sem_inc(acc_stored[s], 16)
                with dve.Fori(0, NG) as i:
                    for o in range(NT):
                        dve.wait_ge(pv_ok, tile_done(i, o))
                        dve.wait_ge(acc_stored[o % 2], (i * (NT // 2) + o // 2 + 1) * 16)
                        nc.vector.tensor_copy(acc[:, o % 2, :], O[:, o % 2, :]).then_inc(acc_ok, 1)

            @block.tensor
            def _(pe):
                pe.sem_inc(pv_ok, NP // 2)

                def score(i, b):
                    o, j, kb, q0 = blocks[b]
                    if j == NT - 1 and kb % NB == 0:
                        pe.wait_ge(op_loaded[kb // NB], (i + 1) * (16 * LOADS))
                    for pair in (2 * b, 2 * b + 1):
                        pe.wait_ge(exp_ok, i * NPAIR + pair + 1)
                        for a in range(2):
                            h = 2 * (pair % 2) + a
                            last = nc.tensor.matmul(S[:, pair % NS, a, 0:TT - q0], k_op[0:ROWS, h, kb * P:(kb + 1) * P],
                                                    q_op[0:ROWS, h, j * TT + q0:(j + 1) * TT], start=True, stop=True)
                        last.then_inc(scored, 1)

                def weigh(i, b):
                    o, j, kb, q0 = blocks[b]
                    if j == NT - 1 and kb % NB == 0:
                        pe.wait_ge(vg_ok, i * NT + NT - kb // NB)
                    first = kb == j * NB
                    if first:
                        pe.wait_ge(acc_ok, i * NT + o + 1)
                    if b >= NBLK - LAG:
                        pe.wait_ge(exp_ok, i * NPAIR + 2 * b + 2 + NS)
                    if kb >= j * NB:
                        pe.wait_ge(cut_ok, i * DIAG + (o * NB + kb - j * NB + 1) * 2)
                    for h in range(HG):
                        last = nc.tensor.matmul(O[h * STRIP:(h + 1) * STRIP, o % 2, q0:TT], vg[:, kb, h, :],
                                                probs[:, (2 * b + h // 2) % NP, h % 2, 0:TT - q0], start=first,
                                                stop=last_of_tile(b), skip_group_check=True)
                    last.then_inc(pv_ok, 1)

                with pe.Fori(0, NG) as i:
                    for b in range(NBLK + LAG):
                        if b < NBLK:
                            score(i, b)
                        if b >= LAG:
                            weigh(i, b - LAG)


def feed(nc, g, d):
    NSTR = 4
    ROUNDS = NT // NSTR
    parts = [("turn_sums0", "PE", 0.6, ()), ("divide0", "DVE", 0.9, ("turn_sums0",)),
             ("turn_sums1", "PE", 0.6, ("divide0",)), ("divide1", "DVE", 0.9, ("turn_sums1",)),
             ("turn_att", "PE", 0.6, ("divide1",)), ("copy_att", "ACT", 1.0, ("turn_att",)),
             ("project", "PE", 3.6, ("copy_att",)), ("stats_att", "DVE", 3.2, ("project",)),
             ("rsqrt_att", "POOL", 2.7, ("stats_att",)), ("norm_att", "ACT", 1.4, ("rsqrt_att",)),
             ("stats_x", "DVE", 3.2, ("norm_att",)), ("rsqrt_x", "POOL", 2.7, ("stats_x",)),
             ("norm_x", "ACT", 1.4, ("rsqrt_x",)), ("turn_h0", "PE", 0.6, ("norm_x",)), ("copy_h0", "ACT", 1.0, ("turn_h0",))]
    for m in range(BLK):
        h_at = f"add{m - 1}" if m else "norm_x"
        parts += [(f"first{m}", "PE", 3.6, (f"copy_h{m}",)), (f"bias_h{m}", "POOL_H", 1.1, (h_at,)),
                  (f"stats{m}", "DVE", 3.2, (f"first{m}",)), (f"rsqrt{m}", "POOL", 2.7, (f"stats{m}",)),
                  (f"norm{m}", "ACT", 1.4, (f"rsqrt{m}",)), (f"turn_norm{m}", "PE", 0.6, (f"norm{m}",)),
                  (f"gelu{m}", "ACT", 1.1, (f"turn_norm{m}",)), (f"second{m}", "PE", 3.6, (f"gelu{m}",)),
                  (f"add{m}", "DVE", 1.3, (f"second{m}", f"bias_h{m}"))]
        if m < BLK - 1:
            parts += [(f"turn_h{m + 1}", "PE", 0.6, (f"add{m}",)), (f"copy_h{m + 1}", "ACT", 1.0, (f"turn_h{m + 1}",))]
    parts += [("stats_h", "DVE", 2.0, (f"add{BLK - 1}",)), ("rsqrt_h", "POOL", 2.7, ("stats_h",)),
              ("norm_h", "ACT", 1.4, ("rsqrt_h",)), ("result", "DVE", 1.2, ("norm_h",))]
    RSQRTS = BLK + 3

    def at(r, part):
        engine = {p[0]: p[1] for p in parts}[part]
        mine = [p[0] for p in parts if p[1] == engine]
        return r * len(mine) + mine.index(part) + 1

    def orders():
        HOP = 0.1
        free = dict(PE=0.0, DVE=0.0, ACT=0.0, POOL=0.0)
        found = {e: [] for e in free}
        end, left = {}, [(k, r, n) for r in range(ROUNDS) for n in range(len(parts)) for k in range(NSTR)]
        while left:
            best = None
            for k, r, n in left:
                name, e, _, after = parts[n]
                before = [(k, r, a) for a in after] + ([(k, r - 1, "result")] if r and not after else [])
                if all(b in end for b in before):
                    start = max([free[e[:4].rstrip("_")]] + [end[b] + HOP for b in before])
                    if best is None or (start, r, n, k) < best:
                        best = (start, r, n, k)
            start, r, n, k = best
            name, e, us, _ = parts[n]
            free[e[:4].rstrip("_")] = end[k, r, name] = start + us
            found[e[:4].rstrip("_")].append((k, r, name))
            left.remove((k, r, n))
        return found

    order = orders()
    with ExitStack() as ctx:
        sem = lambda n: ctx.enter_context(nc.semaphore(n))

        def per_stream(n, s, t=F32):
            return [ctx.enter_context(nc.sbuf_tensor(f"{n}{k}", s, t))[(slice(None),) * len(s)] for k in range(NSTR)]

        acc = per_stream("accC", [P, NG, TT])
        x = per_stream("xC", [P, NB, C])
        u = per_stream("uC", [P, NB, C])
        y = per_stream("yC", [P, NB, C])
        h = per_stream("hC", [P, NB, C])
        hb = per_stream("hbC", [P, NB, C])
        yT = per_stream("yTC", [P, NC, TT])
        st = per_stream("stC", [P, NB, 6])
        mv = per_stream("mvC", [P, NB, 2])
        tmp = per_stream("tmpC", [P, 3, NB])
        rstd = per_stream("rstdC", [P, NB])
        nmr = per_stream("nmrC", [P, NB])
        rl = per_stream("rlC", [P, 2 * H])
        ps = [ctx.enter_context(nc.psum_tensor(f"psC{k}", [P, 2 * TT], F32)) for k in range(NSTR)]
        acc_in, x_in, stored, pe_ok, act_ok, dve_ok, pool_ok, hb_ok, dve_chain, pool_chain = (
            [sem(f"{n}{k}") for k in range(NSTR)]
            for n in ("acc_in", "x_in", "storedC", "pe_ok", "act_ok", "dve_ok", "pool_ok", "hb_ok", "dve_chainC", "pool_chainC"))
        x_tiles = d["x"][0].rearrange("(t b p) c -> t p b c", b=NB, p=P)
        out_tiles = d["out"][0].rearrange("(t b p) c -> t p b c", b=NB, p=P)
        acc_tiles = d["acc"].rearrange("g t p q -> t p g q")

        def repeated(row):
            return row.unsqueeze(1).to_broadcast([P, NB, C])

        with nc.Block() as block:

            @block.sync
            def _(sp):
                for k in range(NSTR):
                    sp.dma_start(acc[k], acc_tiles[k]).then_inc(acc_in[k], 16)
                    sp.dma_start(x[k], x_tiles[k]).then_inc(x_in[k], 16)
                for k, r, part in sorted((x for x in order["PE"] + order["DVE"] if x[2] in ("turn_sums1", "result")),
                                           key=lambda x: (x[1], x[2] == "result")):
                    if part == "turn_sums1" and r + 1 < ROUNDS:
                        sp.wait_ge(pe_ok[k], at(r, part))
                        sp.dma_start(acc[k], acc_tiles[(r + 1) * NSTR + k]).then_inc(acc_in[k], 16)
                    if part == "result":
                        sp.wait_ge(dve_ok[k], at(r, part))
                        sp.dma_start(out_tiles[r * NSTR + k], u[k]).then_inc(stored[k], 16)
                        if r + 1 < ROUNDS:
                            sp.dma_start(x[k], x_tiles[(r + 1) * NSTR + k]).then_inc(x_in[k], 16)
                for k in range(NSTR):
                    sp.wait_ge(stored[k], 16 * ROUNDS)

            @block.tensor
            def _(pe):
                def turn(k, src):
                    for c in range(NC):
                        for b in range(NB):
                            last = nc.tensor.transpose(ps[k][:, c * TT + b * P:c * TT + (b + 1) * P],
                                                       src[:, b, c * P:(c + 1) * P], g["ident"][:, :])
                    last.then_inc(pe_ok[k], 1)

                def product(k, w):
                    for b in range(NB):
                        for c in range(NC):
                            last = nc.tensor.matmul(ps[k][:, b * C:(b + 1) * C], yT[k][:, c, b * P:(b + 1) * P], w[:, c, :],
                                                    start=(c == 0), stop=(c == NC - 1))
                    last.then_inc(pe_ok[k], 1)

                for k, r, part in order["PE"]:
                    if part in ("turn_sums0", "turn_sums1"):
                        half = int(part[-1])
                        if half == 0:
                            pe.wait_ge(acc_in[k], 16 * (r + 1))
                            if r:
                                pe.wait_ge(dve_ok[k], at(r - 1, f"add{BLK - 1}"))
                        else:
                            pe.wait_ge(dve_ok[k], at(r, "divide0"))
                        for b in range(2):
                            q0 = (half * 2 + b) * P
                            for hg in range(NG):
                                last = nc.tensor.transpose(ps[k][:, b * TT + hg * P:b * TT + (hg + 1) * P],
                                                           acc[k][:, hg, q0:q0 + P], g["ident"][:, :])
                        last.then_inc(pe_ok[k], 1)
                    elif part == "turn_att":
                        pe.wait_ge(dve_ok[k], at(r, "divide1"))
                        turn(k, y[k])
                    elif part == "project":
                        pe.wait_ge(act_ok[k], at(r, "copy_att"))
                        product(k, g["wpT"])
                    elif part == "turn_h0":
                        pe.wait_ge(act_ok[k], at(r, "norm_x"))
                        turn(k, h[k])
                    else:
                        m = int(part[-1])
                        if part.startswith("first"):
                            pe.wait_ge(act_ok[k], at(r, f"copy_h{m}"))
                            product(k, g["wfT"][:, 2 * m])
                        elif part.startswith("turn_norm"):
                            pe.wait_ge(act_ok[k], at(r, f"norm{m}"))
                            turn(k, y[k])
                        elif part.startswith("second"):
                            pe.wait_ge(act_ok[k], at(r, f"gelu{m}"))
                            product(k, g["wfT"][:, 2 * m + 1])
                        elif part.startswith("turn_h"):
                            pe.wait_ge(dve_ok[k], at(r, f"add{m - 1}"))
                            turn(k, h[k])

            @block.scalar
            def _(act):
                def normalise(k, dst, src):
                    for b in range(NB):
                        last = nc.scalar.activation(dst[:, b, :], src[:, b, :], ACT.Identity, bias=nmr[k][:, b:b + 1],
                                                    scale=rstd[k][:, b:b + 1])
                    last.then_inc(act_ok[k], 1)

                for k, r, part in order["ACT"]:
                    if part.startswith("copy"):
                        act.wait_ge(pe_ok[k], at(r, part.replace("copy", "turn")))
                        nc.scalar.copy(yT[k], ps[k][:, :].rearrange("p (c t) -> p c t", c=NC)).then_inc(act_ok[k], 1)
                    elif part.startswith("gelu"):
                        m = int(part[-1])
                        act.wait_ge(pe_ok[k], at(r, f"turn_norm{m}"))
                        for c in range(NC):
                            col = m * NC + c
                            last = nc.scalar.activation(yT[k][:, c, :], ps[k][:, c * TT:(c + 1) * TT], ACT.Gelu,
                                                        bias=g["beta"][:, col:col + 1], scale=g["gamma"][:, col:col + 1])
                        last.then_inc(act_ok[k], 1)
                    else:
                        act.wait_ge(pool_ok[k], at(r, part.replace("norm", "rsqrt")))
                        dst, src = dict(norm_att=(y, u), norm_x=(h, x), norm_h=(y, h)).get(part, (y, u))
                        normalise(k, dst[k], src[k])

            @block.gpsimd
            def _(pool):
                calls = [0] * NSTR

                def rsqrt(k):
                    pool_rsqrt(pool, nc, None, pool_chain[k], calls[k] * (RS_OPS - 1), mv[k], tmp[k], rstd[k],
                               nmr[k]).then_inc(pool_ok[k], 1)
                    calls[k] += 1

                for k, r, part in order["POOL"]:
                    if part.startswith("bias_h"):
                        m = int(part[-1])
                        if m == 0:
                            pool.wait_ge(act_ok[k], at(r, "norm_x"))
                        else:
                            pool.wait_ge(dve_ok[k], at(r, f"add{m - 1}"))
                        nc.gpsimd.tensor_tensor(hb[k], h[k], repeated(g["bffn"][:, (2 * m + 1) * C:(2 * m + 2) * C]),
                                                ALU.add).then_inc(hb_ok[k], 1)
                    else:
                        pool.wait_ge(dve_ok[k], at(r, part.replace("rsqrt", "stats")))
                        rsqrt(k)

            @block.vector
            def _(dve):
                links = [0] * NSTR

                def link(k, ins):
                    links[k] += 1
                    ins.then_inc(dve_chain[k], 1)
                    dve.wait_ge(dve_chain[k], links[k])

                def stats(k, src):
                    last = dve_stats(dve, nc, None, dve_chain[k], links[k], src, st[k], mv[k], tmp[k], rstd[k])
                    links[k] += 3
                    last.then_inc(dve_ok[k], 1)

                def evacuate(k, dst, addend):
                    return nc.vector.tensor_tensor(dst, ps[k][:, :].rearrange("p (b c) -> p b c", b=NB), addend, ALU.add)

                for k, r, part in order["DVE"]:
                    if part.startswith("divide"):
                        half = int(part[-1])
                        dve.wait_ge(pe_ok[k], at(r, f"turn_sums{half}"))
                        sums = ps[k][:, :].rearrange("p (n e) -> p n e", e=STRIP)
                        link(k, nc.vector.reciprocal(rl[k], sums[:, :, D]))
                        nc.vector.tensor_tensor(y[k][:, 2 * half:2 * half + 2, :].rearrange("p b (h e) -> p (b h) e", e=D),
                                                sums[:, :, 0:D], bcast(rl[k], D), ALU.mult).then_inc(dve_ok[k], 1)
                    elif part == "stats_att":
                        dve.wait_ge(pe_ok[k], at(r, "project"))
                        if r:
                            dve.wait_ge(stored[k], r * 16)
                        link(k, evacuate(k, u[k], repeated(g["bproj"][:, :])))
                        stats(k, u[k])
                    elif part == "stats_x":
                        dve.wait_ge(x_in[k], 16 * (r + 1))
                        dve.wait_ge(act_ok[k], at(r, "norm_att"))
                        link(k, nc.vector.tensor_tensor(x[k], x[k], y[k], ALU.add))
                        stats(k, x[k])
                    elif part == "stats_h":
                        dve.wait_ge(dve_ok[k], at(r, f"add{BLK - 1}"))
                        stats(k, h[k])
                    elif part.startswith("stats"):
                        m = int(part[-1])
                        dve.wait_ge(pe_ok[k], at(r, f"first{m}"))
                        link(k, evacuate(k, u[k], repeated(g["bffn"][:, 2 * m * C:(2 * m + 1) * C])))
                        stats(k, u[k])
                    elif part.startswith("add"):
                        m = int(part[-1])
                        dve.wait_ge(pe_ok[k], at(r, f"second{m}"))
                        dve.wait_ge(hb_ok[k], at(r, f"bias_h{m}"))
                        evacuate(k, h[k], hb[k]).then_inc(dve_ok[k], 1)
                    elif part == "result":
                        dve.wait_ge(act_ok[k], at(r, "norm_h"))
                        nc.vector.tensor_tensor(u[k], x[k], y[k], ALU.add).then_inc(dve_ok[k], 1)


def build(nc, x, w_attn, b_attn, la_attn, lb_attn, w_proj, b_proj, la_proj, lb_proj, qweights, scales, biases, lora_a,
          lora_b, ln_gamma, ln_beta, out):
    d = dict(x=x, w_attn=w_attn, b_attn=b_attn, la_attn=la_attn, lb_attn=lb_attn, w_proj=w_proj, b_proj=b_proj,
             la_proj=la_proj, lb_proj=lb_proj, qweights=qweights, scales=scales, biases=biases, lora_a=lora_a,
             lora_b=lora_b, ln_gamma=ln_gamma, ln_beta=ln_beta, out=out)
    d["qk_parts"] = nc.dram_tensor("qk_parts", [2, PARTS, C, T], BF16).ap()
    d["shift"] = nc.dram_tensor("shift", [PARTS, H, T], BF16).ap()
    d["acc"] = nc.dram_tensor("acc_sums", [NG, NT, P, TT], F32).ap()
    with ExitStack() as ctx:
        sb = lambda n, s, t=F32: ctx.enter_context(nc.sbuf_tensor(n, s, t))
        g = dict(ident=sb("ident", [P, P]), wqkvT=sb("wqkvT", [P, NC, 3 * C]), wpT=sb("wpT", [P, NC, C]),
                 wfT=sb("wfT", [P, 2 * BLK, NC, C]), bqk=sb("bqk", [P, 2 * NC]), bv=sb("bv", [P, C]),
                 bproj=sb("bproj", [P, C]), bffn=sb("bffn", [P, 2 * BLK * C]), gamma=sb("gamma", [P, BLK * NC]),
                 beta=sb("beta", [P, BLK * NC]), need_max=sb("need_max", [1, 1], I32))
        with ExitStack() as attention:
            for name, shape, dtype in (("v_all", [P, T // P, C], F32), ("q_op", [P, HG, T], BF16), ("k_op", [P, HG, T], BF16),
                                       ("vg", [P, T // P, HG, STRIP], F32)):
                g[name] = attention.enter_context(nc.sbuf_tensor(name, shape, dtype))
            prepare_weights(nc, g, d)
            project(nc, g, d)
            guard(nc, g, d)
            attend(nc, g, d)
        feed(nc, g, d)


_INS = ["L0_attn_x", "L0_attn_w_attn", "L0_attn_b_attn", "L0_attn_la_attn", "L0_attn_lb_attn", "L0_attn_w_proj",
        "L0_attn_b_proj", "L0_attn_la_proj", "L0_attn_lb_proj", "L0_ffn_qweights", "L0_ffn_scales", "L0_ffn_biases",
        "L0_ffn_lora_a", "L0_ffn_lora_b", "L0_ffn_ln_gamma", "L0_ffn_ln_beta"]


def kernel(**inputs):
    import numpy as np
    import concourse.bacc as bacc
    from concourse.bass_utils import run_bass_kernel_spmd

    nc = bacc.Bacc("TRN2", target_bir_lowering=False, num_devices=1)
    arrays, args = {}, []
    for name in _INS:
        a = np.ascontiguousarray(inputs[name])
        arrays[f"in_{name}"] = a
        args.append(nc.dram_tensor(f"in_{name}", a.shape, mybir.dt.from_np(a.dtype), kind="ExternalInput").ap())
    out = nc.dram_tensor("out", [1, T, C], F32, kind="ExternalOutput").ap()
    build(nc, *args, out)
    return run_bass_kernel_spmd(nc, [arrays], core_ids=[0]).results[0]["out"]
```

```python
from contextlib import ExitStack

import concourse.bass as bass
from concourse import mybir

F32 = mybir.dt.float32
BF16 = mybir.dt.bfloat16
I32 = mybir.dt.int32
ALU = mybir.AluOpType
ACT = mybir.ActivationFunctionType
AX = mybir.AxisListType

P = 128
T, C, H = 4096, 256, 16
D = C // H
R = 32
NC = C // P
TT = 512
NB = TT // P
NT = T // TT
HG = 4
NG = H // HG
STRIP = 32
PARTS = 3
Q_PART = (0, 1, 2, 0, 1, 0)
K_PART = (0, 0, 0, 1, 1, 2)
SHIFT0 = D * len(Q_PART)
ROWS = SHIFT0 + PARTS
SCALE = D ** -0.5
EPS = 1e-5
GROUP = 16
BLK = 3
SAFE_SCORE = 40.0
NEG = -1.0e30
RSQRT_SEED = float(0x5F3759DF)
RS_OPS = 11


def bcast(ap, n):
    return ap.unsqueeze(2).to_broadcast([ap.shape[0], ap.shape[1], n])


def hold(eng, sem, value, held):
    eng.wait_ge(sem, value)
    if not isinstance(value, int):
        eng.sem_inc(held, 1)


def pool_rsqrt(pool, nc, held, chain, base, mv, tmp, y, nmr):
    n = 0

    def step(ins):
        nonlocal n
        n += 1
        ins.then_inc(chain, 1)
        hold(pool, chain, base + n, held)

    t, a = tmp[:, 0, :], tmp[:, 2, :]
    step(nc.gpsimd.tensor_tensor(t, y, y, ALU.mult))
    step(nc.gpsimd.tensor_tensor(t, t, tmp[:, 1, :], ALU.mult))
    step(nc.gpsimd.tensor_scalar(t, t, -0.5, 1.5, ALU.mult, ALU.add))
    step(nc.gpsimd.tensor_tensor(y, y, t, ALU.mult))
    step(nc.gpsimd.tensor_tensor(t, y, y, ALU.mult))
    step(nc.gpsimd.tensor_tensor(a, t, tmp[:, 1, :], ALU.mult))
    step(nc.gpsimd.tensor_scalar(t, a, 0.375, -1.25, ALU.mult, ALU.add))
    step(nc.gpsimd.tensor_tensor(t, t, a, ALU.mult))
    step(nc.gpsimd.tensor_scalar(t, t, 1.875, None, ALU.add))
    step(nc.gpsimd.tensor_tensor(y, y, t, ALU.mult))
    n += 1
    assert n == RS_OPS
    return nc.gpsimd.tensor_tensor(nmr, tmp[:, 3, :], y, ALU.mult)


def dve_stats(dve, nc, held, chain, base, src, st, mv, tmp, y):
    for b in range(NB):
        last = nc.vector.bn_stats(st[:, b, :], src[:, b, :])
    last.then_inc(chain, 1)
    hold(dve, chain, base + 1, held)
    for b in range(NB):
        last = nc.vector.bn_aggr(mv[:, b, :], st[:, b, :])
    last.then_inc(chain, 1)
    dve.wait_ge(chain, base + 2)
    nc.vector.tensor_scalar(tmp[:, 3, :], mv[:, :, 0], -1.0, None, ALU.mult)
    nc.vector.tensor_scalar(tmp[:, 1, :], mv[:, :, 1], EPS, None, ALU.add).then_inc(chain, 1)
    dve.wait_ge(chain, base + 3)
    return nc.vector.tensor_scalar(y.bitcast(I32), tmp[:, 1, :].bitcast(I32), -0.5, RSQRT_SEED, ALU.mult, ALU.add)


def x_front(ctx, nc):
    sb = lambda n, s: ctx.enter_context(nc.sbuf_tensor(n, s, F32))
    f = dict(st=sb("stA", [P, 2, NB, 6]), mv=sb("mvA", [P, 2, NB, 2]), tmp=sb("tmpA", [P, 2, 4, NB]),
             rstd=sb("rstdA", [P, 2, NB]), nmr=sb("nmrA", [P, 2, NB]))
    f.update({n: ctx.enter_context(nc.semaphore(n)) for n in ("stats_ok", "rstd_ok", "dve_chainA", "pool_chainA", "heldA")})
    f["x_loaded"] = [ctx.enter_context(nc.semaphore(f"x_loaded{u}")) for u in range(2)]
    return f


def x_stats(dve, nc, g, n, u, loads):
    f = g["front"]
    dve.wait_ge(f["x_loaded"][u], loads * 16)
    dve_stats(dve, nc, f["heldA"], f["dve_chainA"], n * 3, g["x_in"][:, u], f["st"][:, u], f["mv"][:, u],
              f["tmp"][:, u], f["rstd"][:, u]).then_inc(f["stats_ok"], 1)


def x_rsqrt(pool, nc, g, n, u):
    f = g["front"]
    hold(pool, f["stats_ok"], n + 1, f["heldA"])
    pool_rsqrt(pool, nc, f["heldA"], f["pool_chainA"], n * (RS_OPS - 1), f["mv"][:, u], f["tmp"][:, u],
               f["rstd"][:, u], f["nmr"][:, u]).then_inc(f["rstd_ok"], 1)


def prepare_weights(nc, g, d):
    with ExitStack() as ctx:
        sb = lambda n, s, t: ctx.enter_context(nc.sbuf_tensor(n, s, t))
        sem = lambda n: ctx.enter_context(nc.semaphore(n))
        NA, NF = 3 * C // P, 2 * BLK * C // P
        NO = NA + NC + NF
        w_nat = sb("w_nat", [P, NO, C], F32)
        lb_nat = sb("lb_nat", [P, NO, R], F32)
        la = sb("la", [R, 2 + 2 * BLK, C], F32)
        lbT = sb("lbT", [R, NO * P], F32)
        q_int = sb("q_int", [P, NF, C], I32)
        scl = sb("scl", [P, NF, C // GROUP], F32)
        no_shift = sb("no_shift", [P, PARTS * H * T // P], BF16)
        shift_zero, shift_stored = sem("shift_zero"), sem("shift_stored")
        lbT_ps = ctx.enter_context(nc.psum_tensor("lbT_ps", [P, NO * P], F32))
        wT_ps = ctx.enter_context(nc.psum_tensor("wT_ps", [P, 3, 2 * C], F32))
        small_in, w_in, q_in, la_in = sem("small_in"), sem("w_in"), sem("q_in"), sem("la_in")
        zeroed, ident_ok, dequant, transposed, lbT_ok = (sem(n) for n in ("zeroed", "ident_ok", "dequant", "transposed", "lbT_ok"))
        turned_w, lora_ok, wT_ok = sem("turned_w"), sem("lora_ok"), sem("wT_ok")
        mats = [(2 * m, 0, g["wqkvT"][:, :, m * C:(m + 1) * C]) for m in range(3)]
        mats += [(NA, 1, g["wpT"][:, :, :])]
        mats += [(NA + NC + 2 * m, 2 + m, g["wfT"][:, m, :, :]) for m in range(2 * BLK)]
        with nc.Block() as block:

            @block.sync
            def _(sp):
                sp.dma_start(lb_nat[:, 0:NA, :], d["lb_attn"].rearrange("(m p) r -> p m r", p=P)).then_inc(la_in, 16)
                sp.dma_start(lb_nat[:, NA:NA + NC, :], d["lb_proj"].rearrange("(m p) r -> p m r", p=P)).then_inc(la_in, 16)
                sp.dma_start(lb_nat[:, NA + NC:, :], d["lora_b"].rearrange("k (m p) r -> p (k m) r", p=P)).then_inc(la_in, 16)
                sp.dma_start(w_nat[:, 0:NA, :], d["w_attn"].rearrange("(m p) i -> p m i", p=P)).then_inc(w_in, 16)
                sp.dma_start(w_nat[:, NA:NA + NC, :], d["w_proj"].rearrange("(m p) i -> p m i", p=P)).then_inc(w_in, 16)
                sp.dma_start(la[:, 0, :], d["la_attn"]).then_inc(w_in, 16)
                sp.dma_start(la[:, 1, :], d["la_proj"]).then_inc(w_in, 16)
                sp.dma_start(la[:, 2:, :], d["lora_a"].rearrange("k r i -> r k i")).then_inc(w_in, 16)
                for m in range(2 * C // P):
                    sp.dma_start(g["bqk"][:, m:m + 1], d["b_attn"][m * P:(m + 1) * P].rearrange("(p o) -> p o", o=1)).then_inc(small_in, 16)
                for m in range(BLK * NC):
                    at = slice((m % NC) * P, (m % NC + 1) * P)
                    sp.dma_start(g["gamma"][:, m:m + 1], d["ln_gamma"][m // NC, at].rearrange("(p o) -> p o", o=1)).then_inc(small_in, 16)
                    sp.dma_start(g["beta"][:, m:m + 1], d["ln_beta"][m // NC, at].rearrange("(p o) -> p o", o=1)).then_inc(small_in, 16)
                for u in range(2):
                    sp.dma_start(g["x_in"][:, u, :, :], d["x"][0].rearrange("(t b p) c -> t p b c", b=NB, p=P)[u]).then_inc(
                        g["front"]["x_loaded"][u], 16)
                sp.wait_ge(shift_zero, 1)
                sp.dma_start(d["shift"].rearrange("s h t -> (s h t)").rearrange("(p n) -> p n", p=P), no_shift[:, :]).then_inc(shift_stored, 16)
                sp.wait_ge(shift_stored, 16)
                sp.wait_ge(small_in, 16 * (2 * C // P + 2 * BLK * NC + 3))

            @block.scalar
            def _(act):
                act.dma_start(q_int[:, :, :], d["qweights"].rearrange("k (m p) i -> p (k m) i", p=P)).then_inc(q_in, 16)
                act.dma_start(scl[:, :, :], d["scales"].rearrange("k (m p) g -> p (k m) g", p=P)).then_inc(q_in, 16)
                act.dma_start(g["bv"][:, :], d["b_attn"][2 * C:3 * C].rearrange("(o c) -> o c", o=1).to_broadcast([P, C])).then_inc(small_in, 16)
                act.dma_start(g["bproj"][:, :], d["b_proj"].rearrange("(o c) -> o c", o=1).to_broadcast([P, C])).then_inc(small_in, 16)
                act.dma_start(g["bffn"][:, :], d["biases"].rearrange("(o k) c -> o (k c)", o=1).to_broadcast([P, 2 * BLK * C])).then_inc(small_in, 16)
                act.wait_ge(transposed, 1)
                nc.scalar.activation(lbT[:, 0:(NA + NC) * P], lbT_ps[0:R, 0:(NA + NC) * P], ACT.Copy, scale=0.5)
                nc.scalar.activation(lbT[:, (NA + NC) * P:], lbT_ps[0:R, (NA + NC) * P:], ACT.Copy).then_inc(lbT_ok, 1)

                for n in range(2 * len(mats)):
                    act.wait_ge(turned_w, n + 1)
                    nc.scalar.copy(mats[n // 2][2][:, n % 2, :], lbT_ps[:, (n % 3) * TT:(n % 3) * TT + C]).then_inc(lora_ok, 1)

            @block.gpsimd
            def _(pool):
                nc.gpsimd.memset(no_shift[:, :], 0.0).then_inc(shift_zero, 1)
                nc.gpsimd.memset(g["ident"][:, :], 0.0).then_inc(zeroed, 1)
                pool.wait_ge(zeroed, 1)
                nc.gpsimd.affine_select(out=g["ident"][:, :], in_=g["ident"][:, :], compare_op=ALU.not_equal, fill=1.0,
                                        base=0, pattern=[[-1, P]], channel_multiplier=1).then_inc(ident_ok, 1)
                for u in range(2):
                    x_rsqrt(pool, nc, g, u, u)
                pool.wait_ge(g["front"]["rstd_ok"], 2)

            @block.vector
            def _(dve):
                wf = w_nat[:, NA + NC:, :]
                dve.wait_ge(q_in, 32)
                nc.vector.tensor_scalar(wf, q_int[:, :, :], 1.0 / 7.5, -1.0, ALU.mult, ALU.add).then_inc(dequant, 1)
                dve.wait_ge(dequant, 1)
                for m in range(NF):
                    last = nc.vector.tensor_tensor(wf[:, m, :].rearrange("p (g e) -> p g e", e=GROUP),
                                                   wf[:, m, :].rearrange("p (g e) -> p g e", e=GROUP),
                                                   bcast(scl[:, m, :], GROUP), ALU.mult)
                last.then_inc(dequant, 1)
                for n in range(2 * len(mats)):
                    if n in (6, 12):
                        x_stats(dve, nc, g, n // 6 - 1, n // 6 - 1, 1)
                    dve.wait_ge(lora_ok, n + 1)
                    dst = mats[n // 2][2][:, n % 2, :]
                    nc.vector.tensor_tensor(dst, dst, wT_ps[:, n % 3, 0:C], ALU.add).then_inc(wT_ok, 1)

            @block.tensor
            def _(pe):
                pe.wait_ge(ident_ok, 1)
                pe.wait_ge(la_in, 48)
                for m in range(NO):
                    last = nc.tensor.transpose(lbT_ps[0:R, m * P:(m + 1) * P], lb_nat[:, m, :], g["ident"][:, :])
                last.then_inc(transposed, 1)
                pe.wait_ge(w_in, 80)

                def turn_w(n):
                    o0, c = mats[n // 2][0], n % 2
                    if o0 == NA + NC and c == 0:
                        pe.wait_ge(dequant, 2)
                    if n >= 3:
                        pe.wait_ge(wT_ok, n - 2)
                    for o in range(2):
                        nc.tensor.transpose(wT_ps[:, n % 3, o * P:(o + 1) * P], w_nat[:, o0 + o, c * P:(c + 1) * P], g["ident"][:, :])

                for n in range(2 * len(mats)):
                    turn_w(n)
                    if n == 0:
                        pe.wait_ge(lbT_ok, 1)
                    o0, a, _ = mats[n // 2]
                    c = n % 2
                    nc.tensor.matmul(lbT_ps[:, (n % 3) * TT:(n % 3) * TT + C], la[:, a, c * P:(c + 1) * P],
                                     lbT[:, o0 * P:(o0 + 2) * P], start=True, stop=True).then_inc(turned_w, 1)


def project(nc, g, d):
    with ExitStack() as ctx:
        sb = lambda n, s, t: ctx.enter_context(nc.sbuf_tensor(n, s, t))
        ps = lambda n, s: ctx.enter_context(nc.psum_tensor(n, s, F32))
        sem = lambda n: ctx.enter_context(nc.semaphore(n))
        x_in = g["x_in"]
        xn, xnT = (a.rearrange("p g t -> p (g t)") for a in g["acc"][1:3])
        xn = xn.rearrange("p (u b c) -> p u b c", u=2, b=NB)
        xnT = xnT.rearrange("p (u c t) -> p u c t", u=2, c=NC)
        qf = sb("qf", [P, 2, TT], F32)
        res = sb("res", [P, 2, TT], F32)
        parts = sb("parts", [P, 4, PARTS, TT], BF16)
        sq = sb("sq", [P, 4, TT], BF16)
        heads_of = sb("heads_of", [P, STRIP], BF16)
        norms = sb("norms", [P, NT], F32)
        norm_max = sb("norm_max", [P, 1], F32)
        bound = sb("bound", [1, P // 2 + 2], F32)
        psT = ps("psT", [P, NC, TT])
        psQ = ps("psQ", [P, 4, TT])
        psV = ps("psV", [P, NB, C])
        x_loaded, held, rstd, nmr, rstd_ok = (g["front"][n] for n in ("x_loaded", "heldA", "rstd", "nmr", "rstd_ok"))
        stored = [sem(f"stored{m}") for m in range(4)]
        norm_ok, turned, xT_ok = (sem(n) for n in ("norm_ok", "turned", "xT_ok"))
        qk_ok, full_ok, res_ok, split_ok, v_ok, v_out = (sem(n) for n in ("qk_ok", "full_ok", "res_ok", "split_ok", "v_ok", "v_out"))
        x_tiles = d["x"][0].rearrange("(t b p) c -> t p b c", b=NB, p=P)
        ones_ok = sem("ones_ok")
        sel0, sel1, sel_ok, sq_ok, norm_done, norm_read, bound_chain = (
            sem(n) for n in ("sel0", "sel1", "sel_ok", "sq_ok", "norm_done", "norm_read", "bound_chain"))
        SLOTS, BANKS = 2, 4

        def rounds(eng, tile, first=None):
            if first:
                first()
            with eng.Fori(0, NT // 2 - 1) as i:
                for u in range(2):
                    tile(i, u, False)
            for u in range(2):
                tile(NT // 2 - 1, u, u == 1)

        with nc.Block() as block:

            @block.sync
            def _(sp):
                def tile(i, u, last):
                    n = i * 2 + u
                    if not isinstance(i, int):
                        hold(sp, norm_ok, n + 1, held)
                        sp.dma_start(x_in[:, u, :, :], x_tiles[n + 2]).then_inc(x_loaded[u], 16)
                    for m in range(4):
                        hold(sp, split_ok, n * 4 + m + 1 + SLOTS, held)
                        dst = d["qk_parts"][m // 2, :, (m % 2) * P:(m % 2 + 1) * P, bass.ds(n * TT, TT)]
                        sp.dma_start(dst.rearrange("s p t -> p s t"), parts[:, m, :, :]).then_inc(stored[m], 16)

                rounds(sp, tile)
                for m in range(4):
                    sp.wait_ge(stored[m], 16 * (1 + NT))

            @block.scalar
            def _(act):
                for m in range(4):
                    act.sem_inc(stored[m], 16)
                act.sem_inc(full_ok, BANKS)
                act.sem_inc(norm_done, 1)

                def normalise(n, u):
                    act.wait_ge(rstd_ok, n + 1)
                    for b in range(NB):
                        last = nc.scalar.activation(xn[:, u, b, :], x_in[:, u, b, :], ACT.Identity,
                                                    bias=nmr[:, u, b:b + 1], scale=rstd[:, u, b:b + 1])
                    last.then_inc(norm_ok, 1)

                def copy_turned(n, u):
                    act.wait_ge(turned, n + 1)
                    nc.scalar.copy(xnT[:, u, :, :], psT[:, :, :]).then_inc(xT_ok, 1)

                def first():
                    normalise(0, 0)
                    copy_turned(0, 0)

                def tile(i, u, last):
                    n = i * 2 + u
                    for m in range(4):
                        act.wait_ge(qk_ok, n * 4 + m + 1)
                        act.wait_ge(split_ok, n * 4 + m + 1)
                        act.wait_ge(stored[m], (n + 1) * 16)
                        nc.scalar.activation(qf[:, m % 2, :], psQ[:, m, :], ACT.Identity, bias=g["bqk"][:, m:m + 1])
                        if m == 0:
                            act.wait_ge(norm_done, n + 1)
                        nc.scalar.activation(sq[:, m, :], psQ[:, m, :], ACT.Square, bias=g["bqk"][:, m:m + 1]).then_inc(sq_ok, 1)
                        nc.scalar.activation(parts[:, m, 0, :], psQ[:, m, :], ACT.Identity,
                                             bias=g["bqk"][:, m:m + 1]).then_inc(full_ok, 1)
                        if m == 1 and not last:
                            normalise(n + 1, 1 - u)
                    if not last:
                        copy_turned(n + 1, 1 - u)

                rounds(act, tile, first)

            @block.gpsimd
            def _(pool):
                nc.gpsimd.memset(heads_of[:, :], 1.0).then_inc(sel0, 1)
                pool.wait_ge(sel0, 1)
                nc.gpsimd.affine_select(out=heads_of[:, :], in_=heads_of[:, :], compare_op=ALU.is_ge, fill=0.0,
                                        base=0, pattern=[[-D, STRIP]], channel_multiplier=1).then_inc(sel1, 1)
                pool.wait_ge(sel1, 1)
                nc.gpsimd.affine_select(out=heads_of[:, :], in_=heads_of[:, :], compare_op=ALU.is_ge, fill=0.0,
                                        base=D - 1, pattern=[[D, STRIP]], channel_multiplier=-1).then_inc(sel_ok, 1)

                def first():
                    nc.gpsimd.memset(g["vg"][:, :, :, D:STRIP], 1.0).then_inc(ones_ok, 1)
                    pool.wait_ge(ones_ok, 1)
                    nc.gpsimd.memset(g["k_op"][SHIFT0:ROWS, :, :], 1.0).then_inc(ones_ok, 1)
                    pool.wait_ge(ones_ok, 2)

                def tile(i, u, last):
                    if not isinstance(i, int):
                        x_rsqrt(pool, nc, g, i * 2 + u + 2, u)

                rounds(pool, tile, first)

            @block.vector
            def _(dve):
                dve.sem_inc(split_ok, SLOTS)

                def tile(i, u, last):
                    n = i * 2 + u
                    for m in range(4):
                        s = m % 2
                        if m == 1 and not isinstance(i, int):
                            dve.wait_ge(norm_ok, n + 1)
                            x_stats(dve, nc, g, n + 2, u, i + 2)
                        dve.wait_ge(full_ok, n * 4 + m + 1 + BANKS)
                        nc.vector.tensor_tensor(res[:, s, :], qf[:, s, :], parts[:, m, 0, :], ALU.subtract).then_inc(res_ok, 1)
                        dve.wait_ge(res_ok, n * 8 + m * 2 + 1)
                        nc.vector.tensor_copy(parts[:, m, 1, :], res[:, s, :]).then_inc(res_ok, 1)
                        dve.wait_ge(res_ok, n * 8 + m * 2 + 2)
                        nc.vector.tensor_tensor(parts[:, m, 2, :], res[:, s, :], parts[:, m, 1, :], ALU.subtract).then_inc(split_ok, 1)
                    dve.wait_ge(v_ok, n + 1)
                    nc.vector.tensor_tensor(g["v_all"][:, bass.ds(n * NB, NB), :], psV[:, :, :],
                                            g["bv"][:, :].unsqueeze(1).to_broadcast([P, NB, C]), ALU.add).then_inc(v_out, 1)
                    dve.wait_ge(norm_done, n + 1 + 1)
                    nc.vector.reduce_max(norms[:, bass.ds(n, 1)], psQ[:, 3, :], AX.X).then_inc(norm_read, 1)

                rounds(dve, tile)
                dve.wait_ge(norm_read, NT + 1)
                nc.vector.reduce_max(norm_max[:, :], norms[:, :], AX.X).then_inc(bound_chain, 1)
                dve.wait_ge(norm_done, NT + 2)
                nc.vector.tensor_copy(bound[:, 2:], psQ[0:1, 0, 0:P // 2]).then_inc(bound_chain, 1)
                dve.wait_ge(bound_chain, 2)
                nc.vector.tensor_tensor(bound[:, 2:], bound[:, 2:], psQ[0:1, 0, P // 2:P], ALU.mult).then_inc(bound_chain, 1)
                dve.wait_ge(bound_chain, 3)
                nc.vector.reduce_max(bound[:, 0:1], bound[:, 2:], AX.X).then_inc(bound_chain, 1)
                dve.wait_ge(bound_chain, 4)
                nc.vector.tensor_scalar(bound[:, 1:2], bound[:, 0:1], (SAFE_SCORE / SCALE) ** 2, None, ALU.is_le).then_inc(bound_chain, 1)
                dve.wait_ge(bound_chain, 5)
                nc.vector.tensor_scalar(g["need_max"][:, :], bound[:, 1:2], -1.0, 1.0, ALU.mult, ALU.add).then_inc(bound_chain, 1)

            @block.tensor
            def _(pe):
                pe.sem_inc(v_out, 1)
                pe.sem_inc(norm_read, 1)
                pe.wait_ge(sel_ok, 1)

                def turn(n, u):
                    pe.wait_ge(norm_ok, n + 1)
                    for c in range(NC):
                        for b in range(NB):
                            last = nc.tensor.transpose(psT[:, c, b * P:(b + 1) * P], xn[:, u, b, c * P:(c + 1) * P], g["ident"][:, :])
                    last.then_inc(turned, 1)

                def tile(i, u, last):
                    n = i * 2 + u
                    pe.wait_ge(xT_ok, n + 1)
                    for m in range(4):
                        pe.wait_ge(full_ok, n * 4 + m + 1)
                        if m == 3:
                            pe.wait_ge(norm_read, n + 1)
                        for c in range(NC):
                            last_mm = nc.tensor.matmul(psQ[:, m, :], g["wqkvT"][:, c, m * P:(m + 1) * P], xnT[:, u, c, :],
                                                       start=(c == 0), stop=(c == NC - 1))
                        last_mm.then_inc(qk_ok, 1)
                    if not last:
                        turn(n + 1, 1 - u)
                    pe.wait_ge(v_out, n + 1)
                    for b in range(NB):
                        for c in range(NC):
                            last_mm = nc.tensor.matmul(psV[:, b, :], xnT[:, u, c, b * P:(b + 1) * P], g["wqkvT"][:, c, 2 * C:3 * C],
                                                       start=(c == 0), stop=(c == NC - 1))
                    last_mm.then_inc(v_ok, 1)
                    pe.wait_ge(full_ok, n * 4 + 4 + BANKS)
                    for m in range(4):
                        last_mm = nc.tensor.matmul(psQ[m * STRIP:(m + 1) * STRIP, 3, :], heads_of[:, :], sq[:, m, :],
                                                   start=True, stop=True)
                    last_mm.then_inc(norm_done, 1)

                rounds(pe, tile, lambda: turn(0, 0))
                pe.wait_ge(bound_chain, 1)
                nc.tensor.matmul(psQ[0:1, 0, 0:P], norm_max[:, :], g["ident"][:, :], start=True, stop=True).then_inc(norm_done, 1)


def load_parts(eng, d, op, kinds, which, h0, tok, done):
    for r, part in enumerate(kinds):
        src = d["qk_parts"][which, part, bass.ds(h0 * D, HG * D), tok].rearrange("(a e) t -> e a t", e=D)
        eng.dma_start(op[r * D:(r + 1) * D, :, tok], src).then_inc(done, 16)


def guard(nc, g, d):
    QB = T // P
    KEYS = 4 * TT
    chunks = [(b, k) for b in range(QB) for k in range(0, (b + 1) * P, KEYS)]
    NCH = len(chunks)
    STEPS = HG * NCH + 1
    with ExitStack() as ctx:
        sb = lambda n, s, t: ctx.enter_context(nc.sbuf_tensor(n, s, t))
        sem = lambda n: ctx.enter_context(nc.semaphore(n))
        q_op, k_op = g["q_op"], g["k_op"]
        ident_b = sb("ident_b", [P, P], BF16)
        unseen = sb("unseen", [P, P], BF16)
        mx = sb("mx", [P, 2, HG * QB], F32)
        top = sb("top", [P, HG * QB], F32)
        neg = sb("neg", [P, P], F32)
        rest = sb("rest", [P, P], F32)
        sh = sb("sh", [P, PARTS, P], BF16)
        S = ctx.enter_context(nc.psum_tensor("SG", [P, 2, KEYS], F32))
        op_loaded, op_used, scored, reduced, tops_ok = (sem(n) for n in ("op_loadedG", "op_used", "scored", "reduced", "tops_ok"))
        z_ok, masks_ok, chain, sh_ok, sh_stored = (sem(n) for n in ("z_ok", "masks_ok", "chainG", "sh_ok", "sh_stored"))
        held = sem("heldG")
        shift_rows = d["shift"].rearrange("s (g a) (b q) -> g (a b) s q", a=HG, q=P)
        LOADS = len(Q_PART) + len(K_PART)
        with nc.Block() as block:

            @block.sync
            def _(sp):
                need = sp.value_load(g["need_max"][0:1, 0:1], min_val=0, max_val=1)
                with sp.If(need == 1):
                    sp.sem_inc(op_used, 1)
                    with sp.Fori(0, NG) as i:
                        hold(sp, op_used, i + 1, held)
                        load_parts(sp, d, q_op, Q_PART, 0, i * HG, slice(0, T), op_loaded)
                        load_parts(sp, d, k_op, K_PART, 1, i * HG, slice(0, T), op_loaded)

            @block.scalar
            def _(act):
                need = act.value_load(g["need_max"][0:1, 0:1], min_val=0, max_val=1)
                with act.If(need == 1):
                    act.sem_inc(sh_stored, 16)
                    with act.Fori(0, NG) as i:
                        act.wait_ge(sh_ok, i + 1)
                        act.dma_start(shift_rows[i], sh[:, :, :]).then_inc(sh_stored, 16)
                    act.wait_ge(sh_stored, 16 * (NG + 1))

            @block.gpsimd
            def _(pool):
                need = pool.value_load(g["need_max"][0:1, 0:1], min_val=0, max_val=1)
                with pool.If(need == 1):
                    nc.gpsimd.memset(ident_b[:, :], 0.0).then_inc(z_ok, 1)
                    nc.gpsimd.memset(unseen[:, :], 0.0).then_inc(z_ok, 1)
                    pool.wait_ge(z_ok, 2)
                    nc.gpsimd.affine_select(out=ident_b[:, :], in_=ident_b[:, :], compare_op=ALU.not_equal, fill=1.0,
                                            base=0, pattern=[[-1, P]], channel_multiplier=1).then_inc(masks_ok, 1)
                    nc.gpsimd.affine_select(out=unseen[:, :], in_=unseen[:, :], compare_op=ALU.is_ge, fill=NEG,
                                            base=0, pattern=[[-1, P]], channel_multiplier=1).then_inc(masks_ok, 1)

            @block.vector
            def _(dve):
                need = dve.value_load(g["need_max"][0:1, 0:1], min_val=0, max_val=1)
                with dve.If(need == 1):
                    dve.sem_inc(reduced, 2)
                    nc.vector.memset(mx[:, 1, :], 3.0 * NEG).then_inc(chain, 1)
                    dve.wait_ge(chain, 1)
                    with dve.Fori(0, NG) as i:
                        with dve.Fori(0, HG) as a:
                            for c, (b, k) in enumerate(chunks):
                                w = min(KEYS, (b + 1) * P - k)
                                dve.wait_ge(scored, i * STEPS + a * NCH + c + 1)
                                nc.vector.reduce_max(mx[:, k // KEYS, bass.ds(a * QB + b, 1)], S[:, c % 2, 0:w], AX.X).then_inc(reduced, 1)
                        dve.wait_ge(reduced, i * STEPS + HG * NCH + 2)
                        nc.vector.tensor_tensor(top[:, :], mx[:, 0, :], mx[:, 1, :], ALU.max).then_inc(tops_ok, 1)
                        dve.wait_ge(scored, i * STEPS + STEPS)
                        nc.vector.tensor_scalar(neg[:, :], S[:, 0, 0:P], -1.0, None, ALU.mult).then_inc(reduced, 1)
                        dve.wait_ge(reduced, i * STEPS + STEPS + 2)
                        dve.wait_ge(sh_stored, i * 16 + 16)
                        nc.vector.tensor_copy(sh[:, 0, :], neg[:, :]).then_inc(chain, 1)
                        dve.wait_ge(chain, i * 4 + 2)
                        nc.vector.tensor_tensor(rest[:, :], neg[:, :], sh[:, 0, :], ALU.subtract).then_inc(chain, 1)
                        dve.wait_ge(chain, i * 4 + 3)
                        nc.vector.tensor_copy(sh[:, 1, :], rest[:, :]).then_inc(chain, 1)
                        dve.wait_ge(chain, i * 4 + 4)
                        nc.vector.tensor_tensor(sh[:, 2, :], rest[:, :], sh[:, 1, :], ALU.subtract).then_inc(sh_ok, 1)
                        dve.sem_inc(chain, 1)

            @block.tensor
            def _(pe):
                need = pe.value_load(g["need_max"][0:1, 0:1], min_val=0, max_val=1)
                with pe.If(need == 1):
                    pe.wait_ge(masks_ok, 2)
                    with pe.Fori(0, NG) as i:
                        pe.wait_ge(op_loaded, i * (LOADS * 16) + LOADS * 16)
                        hold(pe, reduced, i * STEPS + 2, held)
                        with pe.Fori(0, HG) as a:
                            for c, (b, k) in enumerate(chunks):
                                pe.wait_ge(reduced, i * STEPS + a * NCH + c + 1)
                                end = (b + 1) * P
                                for k0 in range(k, min(k + KEYS, end), TT):
                                    w = min(TT, end - k0)
                                    diag = k0 + w == end
                                    last = nc.tensor.matmul(S[:, c % 2, k0 - k:k0 - k + w], q_op[0:SHIFT0, a, b * P:(b + 1) * P],
                                                            k_op[0:SHIFT0, a, k0:k0 + w], start=True, stop=not diag)
                                    if diag:
                                        last = nc.tensor.matmul(S[:, c % 2, end - P - k:end - k], ident_b[:, :], unseen[:, :],
                                                                start=False, stop=True)
                                last.then_inc(scored, 1)
                        pe.wait_ge(tops_ok, i + 1)
                        nc.tensor.transpose(S[:, 0, 0:P], top[:, :], g["ident"][:, :]).then_inc(scored, 1)
                        pe.sem_inc(op_used, 1)


def attend(nc, g, d):
    with ExitStack() as ctx:
        sb = lambda n, s, t: ctx.enter_context(nc.sbuf_tensor(n, s, t))
        sem = lambda n: ctx.enter_context(nc.semaphore(n))
        NS, NP = 3, 6
        q_op, k_op, vg = g["q_op"], g["k_op"], g["vg"]
        probs = sb("probs", [P, NP, 2, TT], F32)
        acc = sb("acc", [P, 2, TT], F32)
        KEPT = len(g["acc"])
        S = ctx.enter_context(nc.psum_tensor("S", [P, NS, 2, TT], F32))
        O = ctx.enter_context(nc.psum_tensor("O", [P, 2, TT], F32))
        held = sem("heldB")
        op_loaded = [sem(f"op_loaded{s}") for s in range(NT)]
        acc_stored = [sem(f"acc_stored{s}") for s in range(2)]
        vg_ok, scored, exp_ok, cut_ok, pv_ok, acc_ok = (
            sem(n) for n in ("vg_ok", "scoredB", "exp_ok", "cut_ok", "pv_ok", "acc_ok"))
        LOADS = len(Q_PART) + len(K_PART) + 1

        blocks = []
        for o, j in enumerate(range(NT - 1, -1, -1)):
            blocks += [(o, j, j * NB + b, b * P) for b in range(NB)]
            blocks += [(o, j, s * NB + b, 0) for s in range(j - 1, -1, -1) for b in range(NB)]
        NBLK = len(blocks)
        NPAIR = 2 * NBLK
        DIAG = 2 * NB * NT
        LAG = 2
        assert NPAIR % NS == 0 and NPAIR % NP == 0 and NT % 2 == 0

        def last_of_tile(n):
            return n + 1 == NBLK or blocks[n + 1][0] != blocks[n][0]

        def tile_done(i, o):
            return i * NBLK + sum(x[0] <= o for x in blocks) + NP // 2

        with nc.Block() as block:

            @block.sync
            def _(sp):
                def load(i, s):
                    tok = slice(s * TT, (s + 1) * TT)
                    load_parts(sp, d, q_op, Q_PART, 0, i * HG, tok, op_loaded[s])
                    load_parts(sp, d, k_op, K_PART, 1, i * HG, tok, op_loaded[s])
                    sp.dma_start(q_op[SHIFT0:ROWS, :, tok], d["shift"][:, bass.ds(i * HG, HG), tok]).then_inc(op_loaded[s], 16)

                def store(i, o):
                    hold(sp, acc_ok, i * NT + o + 1 + 2, held)
                    sp.dma_start(d["acc"][i, NT - 1 - o], acc[:, o % 2, :]).then_inc(acc_stored[o % 2], 16)

                for o in range(NT):
                    load(0, NT - 1 - o)
                with sp.Fori(1, NG) as i:
                    for o in range(NT):
                        hold(sp, pv_ok, tile_done(i - 1, o), held)
                        load(i, NT - 1 - o)
                        if o >= KEPT:
                            store(i - 1, o)
                for o in range(KEPT, NT):
                    store(NG - 1, o)
                for s in range(2):
                    sp.wait_ge(acc_stored[s], 16 * (1 + NG * (NT - KEPT) // 2))

            @block.gpsimd
            def _(pool):
                def take_v(i, o):
                    s = NT - 1 - o
                    at = slice(s * NB, (s + 1) * NB)
                    nc.gpsimd.tensor_copy(vg[:, at, :, 0:D], g["v_all"][:, at, bass.ds(i * (HG * D), HG * D)]
                                          .rearrange("p b (a e) -> p b a e", e=D)).then_inc(vg_ok, 1)

                def cut(i):
                    n = 0
                    for b, (o, j, kb, q0) in enumerate(blocks):
                        if kb < j * NB:
                            continue
                        for pair in (2 * b, 2 * b + 1):
                            hold(pool, exp_ok, i * NPAIR + pair + 1 + NS, held)
                            tri = probs[:, pair % NP, :, 0:P]
                            nc.gpsimd.affine_select(out=tri, in_=tri, compare_op=ALU.is_ge, fill=0.0, base=0,
                                                    pattern=[[0, 2], [1, P]], channel_multiplier=-1).then_inc(cut_ok, 1)
                            n += 1
                    assert n == DIAG

                for o in range(NT):
                    take_v(0, o)
                with pool.Fori(0, NG - 1) as i:
                    cut(i)
                    for o in range(NT):
                        pool.wait_ge(pv_ok, tile_done(i, o))
                        take_v(i + 1, o)
                cut(NG - 1)

            @block.scalar
            def _(act):
                act.sem_inc(exp_ok, NS)
                with act.Fori(0, NG) as i:
                    for b, (o, j, kb, q0) in enumerate(blocks):
                        for pair in (2 * b, 2 * b + 1):
                            act.wait_ge(scored, i * NPAIR + pair + 1)
                            act.wait_ge(pv_ok, i * NBLK + b - NP // 2 + 1 + NP // 2)
                            nc.scalar.activation(probs[:, pair % NP, :, 0:TT - q0], S[:, pair % NS, :, 0:TT - q0], ACT.Exp,
                                                 scale=SCALE).then_inc(exp_ok, 1)

            @block.vector
            def _(dve):
                dve.sem_inc(acc_ok, 2)
                for s in range(2):
                    dve.sem_inc(acc_stored[s], 16)
                with dve.Fori(0, NG) as i:
                    for o in range(NT):
                        dve.wait_ge(pv_ok, tile_done(i, o))
                        if o < KEPT:
                            nc.vector.tensor_copy(g["acc"][o][:, bass.ds(i, 1), :], O[:, o % 2:o % 2 + 1, :]).then_inc(acc_ok, 1)
                            continue
                        dve.wait_ge(acc_stored[o % 2], (i * ((NT - KEPT) // 2) + (o - KEPT) // 2 + 1) * 16)
                        nc.vector.tensor_copy(acc[:, o % 2, :], O[:, o % 2, :]).then_inc(acc_ok, 1)

            @block.tensor
            def _(pe):
                pe.sem_inc(pv_ok, NP // 2)

                def score(i, b):
                    o, j, kb, q0 = blocks[b]
                    if j == NT - 1 and kb % NB == 0:
                        pe.wait_ge(op_loaded[kb // NB], (i + 1) * (16 * LOADS))
                    for pair in (2 * b, 2 * b + 1):
                        pe.wait_ge(exp_ok, i * NPAIR + pair + 1)
                        for a in range(2):
                            h = 2 * (pair % 2) + a
                            last = nc.tensor.matmul(S[:, pair % NS, a, 0:TT - q0], k_op[0:ROWS, h, kb * P:(kb + 1) * P],
                                                    q_op[0:ROWS, h, j * TT + q0:(j + 1) * TT], start=True, stop=True)
                        last.then_inc(scored, 1)

                def weigh(i, b):
                    o, j, kb, q0 = blocks[b]
                    if j == NT - 1 and kb % NB == 0:
                        pe.wait_ge(vg_ok, i * NT + NT - kb // NB)
                    first = kb == j * NB
                    if first:
                        pe.wait_ge(acc_ok, i * NT + o + 1)
                    if b >= NBLK - LAG:
                        pe.wait_ge(exp_ok, i * NPAIR + 2 * b + 2 + NS)
                    if kb >= j * NB:
                        pe.wait_ge(cut_ok, i * DIAG + (o * NB + kb - j * NB + 1) * 2)
                    for h in range(HG):
                        last = nc.tensor.matmul(O[h * STRIP:(h + 1) * STRIP, o % 2, q0:TT], vg[:, kb, h, :],
                                                probs[:, (2 * b + h // 2) % NP, h % 2, 0:TT - q0], start=first,
                                                stop=last_of_tile(b), skip_group_check=True)
                    last.then_inc(pv_ok, 1)

                with pe.Fori(0, NG) as i:
                    for b in range(NBLK + LAG):
                        if b < NBLK:
                            score(i, b)
                        if b >= LAG:
                            weigh(i, b - LAG)


def feed(nc, g, d):
    NSTR = len(g["acc"])
    ROUNDS = NT // NSTR
    parts = [("turn_sums0", "PE", 0.9, ()), ("divide0", "DVE", 0.95, ("turn_sums0",)),
             ("turn_sums1", "PE", 0.9, ("divide0",)), ("divide1", "DVE", 0.95, ("turn_sums1",)),
             ("turn_att", "PE", 0.9, ("divide1",)), ("copy_att", "ACT", 0.95, ("turn_att",)),
             ("project", "PE", 3.45, ("copy_att",)), ("stats_att", "DVE", 3.55, ("project",)),
             ("rsqrt_att", "POOL", 2.9, ("stats_att",)), ("norm_att", "ACT", 2.0, ("rsqrt_att",)),
             ("stats_x", "DVE", 3.55, ("norm_att",)), ("rsqrt_x", "POOL", 2.9, ("stats_x",)),
             ("norm_x", "ACT", 2.0, ("rsqrt_x",)), ("turn_h0", "PE", 0.9, ("norm_x",)), ("copy_h0", "ACT", 0.95, ("turn_h0",))]
    for m in range(BLK):
        h_at = f"add{m - 1}" if m else "norm_x"
        parts += [(f"first{m}", "PE", 3.45, (f"copy_h{m}",)), (f"bias_h{m}", "POOL_H", 2.3, (h_at,)),
                  (f"stats{m}", "DVE", 3.55, (f"first{m}",)), (f"rsqrt{m}", "POOL", 2.9, (f"stats{m}",)),
                  (f"norm{m}", "ACT", 2.0, (f"rsqrt{m}",)), (f"turn_norm{m}", "PE", 0.9, (f"norm{m}",)),
                  (f"gelu{m}", "ACT", 1.35, (f"turn_norm{m}",)), (f"second{m}", "PE", 3.45, (f"gelu{m}",)),
                  (f"add{m}", "DVE", 1.2, (f"second{m}", f"bias_h{m}"))]
        if m < BLK - 1:
            parts += [(f"turn_h{m + 1}", "PE", 0.9, (f"add{m}",)), (f"copy_h{m + 1}", "ACT", 0.95, (f"turn_h{m + 1}",))]
    parts += [("stats_h", "DVE", 2.4, (f"add{BLK - 1}",)), ("rsqrt_h", "POOL", 2.9, ("stats_h",)),
              ("norm_h", "ACT", 2.0, ("rsqrt_h",)), ("result", "DVE", 1.15, ("norm_h",))]

    def at(r, part):
        engine = {p[0]: p[1] for p in parts}[part]
        mine = [p[0] for p in parts if p[1] == engine]
        return r * len(mine) + mine.index(part) + 1

    def orders():
        HOP = 0.1
        BACK = ((0, 10, 32, 32), (36, 36, 38, 18))
        way = {}
        for name, _, us, _ in reversed(parts):
            way[name] = us + max([way[p[0]] for p in parts if name in p[3]] + [0.0])
        free = dict(PE=0.0, DVE=0.0, ACT=0.0, POOL=0.0)
        found = {e: [] for e in free}
        end, left = {}, [(k, r, n) for r in range(ROUNDS) for n in range(len(parts)) for k in range(NSTR)]
        while left:
            best = None
            for k, r, n in left:
                name, e, _, after = parts[n]
                before = [(k, r, a) for a in after]
                if r and not after:
                    before.append((k, r - 1, f"add{BLK - 1}"))
                if r and name == "divide0":
                    before.append((k, r - 1, "result"))
                if all(b in end for b in before):
                    start = max([free[e[:4].rstrip("_")]] + [end[b] + HOP for b in before])
                    rank = (start, BACK[r][k] - way[name], k, r, n)
                    if best is None or rank < best:
                        best = rank
            start, _, k, r, n = best
            name, e, us, _ = parts[n]
            free[e[:4].rstrip("_")] = end[k, r, name] = start + us
            found[e[:4].rstrip("_")].append((k, r, name))
            left.remove((k, r, n))
        return found

    order = orders()
    with ExitStack() as ctx:
        sem = lambda n: ctx.enter_context(nc.semaphore(n))

        def per_stream(n, s, t=F32):
            return [ctx.enter_context(nc.sbuf_tensor(f"{n}{k}", s, t))[(slice(None),) * len(s)] for k in range(NSTR)]

        acc = g["acc"]
        x = per_stream("xC", [P, NB, C])
        u = per_stream("uC", [P, NB, C])
        y = per_stream("yC", [P, NB, C])
        h = per_stream("hC", [P, NB, C])
        hb = per_stream("hbC", [P, NB, C])
        yT = per_stream("yTC", [P, NC, TT])
        st = per_stream("stC", [P, NB, 6])
        mv = per_stream("mvC", [P, NB, 2])
        tmp = per_stream("tmpC", [P, 4, NB])
        rstd = per_stream("rstdC", [P, NB])
        nmr = per_stream("nmrC", [P, NB])
        rl = per_stream("rlC", [P, 2 * H])
        ps = [ctx.enter_context(nc.psum_tensor(f"psC{k}", [P, 2 * TT], F32)) for k in range(NSTR)]
        acc_in, x_in, stored, pe_ok, act_ok, dve_ok, pool_ok, hb_ok, dve_chain, pool_chain = (
            [sem(f"{n}{k}") for k in range(NSTR)]
            for n in ("acc_in", "x_in", "storedC", "pe_ok", "act_ok", "dve_ok", "pool_ok", "hb_ok", "dve_chainC", "pool_chainC"))
        x_tiles = d["x"][0].rearrange("(t b p) c -> t p b c", b=NB, p=P)
        out_tiles = d["out"][0].rearrange("(t b p) c -> t p b c", b=NB, p=P)
        acc_tiles = d["acc"].rearrange("g t p q -> t p g q")

        def tile(k, r):
            return NT - 1 - (r * NSTR + k)

        def repeated(row):
            return row.unsqueeze(1).to_broadcast([P, NB, C])

        with nc.Block() as block:

            @block.sync
            def _(sp):
                for k in range(NSTR):
                    sp.dma_start(x[k], x_tiles[tile(k, 0)]).then_inc(x_in[k], 16)
                for k, r, part in sorted((x for x in order["PE"] + order["DVE"] if x[2] in ("turn_sums1", "result")),
                                           key=lambda x: (x[1], x[2] == "result")):
                    if part == "turn_sums1" and r + 1 < ROUNDS:
                        sp.wait_ge(pe_ok[k], at(r, part))
                        sp.dma_start(acc[k], acc_tiles[tile(k, r + 1)]).then_inc(acc_in[k], 16)
                    if part == "result":
                        sp.wait_ge(dve_ok[k], at(r, part))
                        sp.dma_start(out_tiles[tile(k, r)], u[k]).then_inc(stored[k], 16)
                        if r + 1 < ROUNDS:
                            sp.dma_start(x[k], x_tiles[tile(k, r + 1)]).then_inc(x_in[k], 16)
                for k in range(NSTR):
                    sp.wait_ge(stored[k], 16 * ROUNDS)

            @block.tensor
            def _(pe):
                def turn(k, src):
                    for c in range(NC):
                        for b in range(NB):
                            last = nc.tensor.transpose(ps[k][:, c * TT + b * P:c * TT + (b + 1) * P],
                                                       src[:, b, c * P:(c + 1) * P], g["ident"][:, :])
                    last.then_inc(pe_ok[k], 1)

                def product(k, w):
                    for b in range(NB):
                        for c in range(NC):
                            last = nc.tensor.matmul(ps[k][:, b * C:(b + 1) * C], yT[k][:, c, b * P:(b + 1) * P], w[:, c, :],
                                                    start=(c == 0), stop=(c == NC - 1))
                    last.then_inc(pe_ok[k], 1)

                for k, r, part in order["PE"]:
                    if part in ("turn_sums0", "turn_sums1"):
                        half = int(part[-1])
                        if half == 0:
                            if r:
                                pe.wait_ge(acc_in[k], 16 * r)
                                pe.wait_ge(dve_ok[k], at(r - 1, f"add{BLK - 1}"))
                        else:
                            pe.wait_ge(dve_ok[k], at(r, "divide0"))
                        for b in range(2):
                            q0 = (half * 2 + b) * P
                            for hg in range(NG):
                                last = nc.tensor.transpose(ps[k][:, b * TT + hg * P:b * TT + (hg + 1) * P],
                                                           acc[k][:, hg, q0:q0 + P], g["ident"][:, :])
                        last.then_inc(pe_ok[k], 1)
                    elif part == "turn_att":
                        pe.wait_ge(dve_ok[k], at(r, "divide1"))
                        turn(k, y[k])
                    elif part == "project":
                        pe.wait_ge(act_ok[k], at(r, "copy_att"))
                        product(k, g["wpT"])
                    elif part == "turn_h0":
                        pe.wait_ge(act_ok[k], at(r, "norm_x"))
                        turn(k, h[k])
                    else:
                        m = int(part[-1])
                        if part.startswith("first"):
                            pe.wait_ge(act_ok[k], at(r, f"copy_h{m}"))
                            product(k, g["wfT"][:, 2 * m])
                        elif part.startswith("turn_norm"):
                            pe.wait_ge(act_ok[k], at(r, f"norm{m}"))
                            turn(k, y[k])
                        elif part.startswith("second"):
                            pe.wait_ge(act_ok[k], at(r, f"gelu{m}"))
                            product(k, g["wfT"][:, 2 * m + 1])
                        elif part.startswith("turn_h"):
                            pe.wait_ge(dve_ok[k], at(r, f"add{m - 1}"))
                            turn(k, h[k])

            @block.scalar
            def _(act):
                def normalise(k, dst, src):
                    for b in range(NB):
                        last = nc.scalar.activation(dst[:, b, :], src[:, b, :], ACT.Identity, bias=nmr[k][:, b:b + 1],
                                                    scale=rstd[k][:, b:b + 1])
                    last.then_inc(act_ok[k], 1)

                for k, r, part in order["ACT"]:
                    if part.startswith("copy"):
                        act.wait_ge(pe_ok[k], at(r, part.replace("copy", "turn")))
                        nc.scalar.copy(yT[k], ps[k][:, :].rearrange("p (c t) -> p c t", c=NC)).then_inc(act_ok[k], 1)
                    elif part.startswith("gelu"):
                        m = int(part[-1])
                        act.wait_ge(pe_ok[k], at(r, f"turn_norm{m}"))
                        for c in range(NC):
                            col = m * NC + c
                            last = nc.scalar.activation(yT[k][:, c, :], ps[k][:, c * TT:(c + 1) * TT], ACT.Gelu,
                                                        bias=g["beta"][:, col:col + 1], scale=g["gamma"][:, col:col + 1])
                        last.then_inc(act_ok[k], 1)
                    else:
                        act.wait_ge(pool_ok[k], at(r, part.replace("norm", "rsqrt")))
                        dst, src = dict(norm_att=(y, u), norm_x=(h, x), norm_h=(y, h)).get(part, (y, u))
                        normalise(k, dst[k], src[k])

            @block.gpsimd
            def _(pool):
                calls = [0] * NSTR

                def rsqrt(k):
                    pool_rsqrt(pool, nc, None, pool_chain[k], calls[k] * (RS_OPS - 1), mv[k], tmp[k], rstd[k],
                               nmr[k]).then_inc(pool_ok[k], 1)
                    calls[k] += 1

                for k, r, part in order["POOL"]:
                    if part.startswith("bias_h"):
                        m = int(part[-1])
                        if m == 0:
                            pool.wait_ge(act_ok[k], at(r, "norm_x"))
                        else:
                            pool.wait_ge(dve_ok[k], at(r, f"add{m - 1}"))
                        nc.gpsimd.tensor_tensor(hb[k], h[k], repeated(g["bffn"][:, (2 * m + 1) * C:(2 * m + 2) * C]),
                                                ALU.add).then_inc(hb_ok[k], 1)
                    else:
                        pool.wait_ge(dve_ok[k], at(r, part.replace("rsqrt", "stats")))
                        rsqrt(k)

            @block.vector
            def _(dve):
                links = [0] * NSTR

                def link(k, ins):
                    links[k] += 1
                    ins.then_inc(dve_chain[k], 1)
                    dve.wait_ge(dve_chain[k], links[k])

                def stats(k, src):
                    last = dve_stats(dve, nc, None, dve_chain[k], links[k], src, st[k], mv[k], tmp[k], rstd[k])
                    links[k] += 3
                    last.then_inc(dve_ok[k], 1)

                def evacuate(k, dst, addend):
                    return nc.vector.tensor_tensor(dst, ps[k][:, :].rearrange("p (b c) -> p b c", b=NB), addend, ALU.add)

                for k, r, part in order["DVE"]:
                    if part.startswith("divide"):
                        half = int(part[-1])
                        dve.wait_ge(pe_ok[k], at(r, f"turn_sums{half}"))
                        sums = ps[k][:, :].rearrange("p (n e) -> p n e", e=STRIP)
                        link(k, nc.vector.reciprocal(rl[k], sums[:, :, D]))
                        nc.vector.tensor_tensor(y[k][:, 2 * half:2 * half + 2, :].rearrange("p b (h e) -> p (b h) e", e=D),
                                                sums[:, :, 0:D], bcast(rl[k], D), ALU.mult).then_inc(dve_ok[k], 1)
                    elif part == "stats_att":
                        dve.wait_ge(pe_ok[k], at(r, "project"))
                        if r:
                            dve.wait_ge(stored[k], r * 16)
                        link(k, evacuate(k, u[k], repeated(g["bproj"][:, :])))
                        stats(k, u[k])
                    elif part == "stats_x":
                        dve.wait_ge(x_in[k], 16 * (r + 1))
                        dve.wait_ge(act_ok[k], at(r, "norm_att"))
                        link(k, nc.vector.tensor_tensor(x[k], x[k], y[k], ALU.add))
                        stats(k, x[k])
                    elif part == "stats_h":
                        dve.wait_ge(dve_ok[k], at(r, f"add{BLK - 1}"))
                        stats(k, h[k])
                    elif part.startswith("stats"):
                        m = int(part[-1])
                        dve.wait_ge(pe_ok[k], at(r, f"first{m}"))
                        link(k, evacuate(k, u[k], repeated(g["bffn"][:, 2 * m * C:(2 * m + 1) * C])))
                        stats(k, u[k])
                    elif part.startswith("add"):
                        m = int(part[-1])
                        dve.wait_ge(pe_ok[k], at(r, f"second{m}"))
                        dve.wait_ge(hb_ok[k], at(r, f"bias_h{m}"))
                        evacuate(k, h[k], hb[k]).then_inc(dve_ok[k], 1)
                    elif part == "result":
                        dve.wait_ge(act_ok[k], at(r, "norm_h"))
                        nc.vector.tensor_tensor(u[k], x[k], y[k], ALU.add).then_inc(dve_ok[k], 1)


def build(nc, x, w_attn, b_attn, la_attn, lb_attn, w_proj, b_proj, la_proj, lb_proj, qweights, scales, biases, lora_a,
          lora_b, ln_gamma, ln_beta, out):
    d = dict(x=x, w_attn=w_attn, b_attn=b_attn, la_attn=la_attn, lb_attn=lb_attn, w_proj=w_proj, b_proj=b_proj,
             la_proj=la_proj, lb_proj=lb_proj, qweights=qweights, scales=scales, biases=biases, lora_a=lora_a,
             lora_b=lora_b, ln_gamma=ln_gamma, ln_beta=ln_beta, out=out)
    d["qk_parts"] = nc.dram_tensor("qk_parts", [2, PARTS, C, T], BF16).ap()
    d["shift"] = nc.dram_tensor("shift", [PARTS, H, T], BF16).ap()
    d["acc"] = nc.dram_tensor("acc_sums", [NG, NT, P, TT], F32).ap()
    with ExitStack() as ctx:
        sb = lambda n, s, t=F32: ctx.enter_context(nc.sbuf_tensor(n, s, t))
        g = dict(ident=sb("ident", [P, P]), wqkvT=sb("wqkvT", [P, NC, 3 * C]), wpT=sb("wpT", [P, NC, C]),
                 wfT=sb("wfT", [P, 2 * BLK, NC, C]), bqk=sb("bqk", [P, 2 * NC]), bv=sb("bv", [P, C]),
                 bproj=sb("bproj", [P, C]), bffn=sb("bffn", [P, 2 * BLK * C]), gamma=sb("gamma", [P, BLK * NC]),
                 beta=sb("beta", [P, BLK * NC]), need_max=sb("need_max", [1, 1], I32))
        g["acc"] = [sb(f"acc{k}", [P, NG, TT])[:, :, :] for k in range(NT // 2)]
        g["x_in"] = g["acc"][0].rearrange("p g t -> p (g t)").rearrange("p (u b c) -> p u b c", u=2, b=NB)
        g["front"] = x_front(ctx, nc)
        prepare_weights(nc, g, d)
        with ExitStack() as attention:
            for name, shape, dtype in (("v_all", [P, T // P, C], F32), ("q_op", [P, HG, T], BF16), ("k_op", [P, HG, T], BF16),
                                       ("vg", [P, T // P, HG, STRIP], F32)):
                g[name] = attention.enter_context(nc.sbuf_tensor(name, shape, dtype))
            project(nc, g, d)
            guard(nc, g, d)
            attend(nc, g, d)
        feed(nc, g, d)


_INS = ["L0_attn_x", "L0_attn_w_attn", "L0_attn_b_attn", "L0_attn_la_attn", "L0_attn_lb_attn", "L0_attn_w_proj",
        "L0_attn_b_proj", "L0_attn_la_proj", "L0_attn_lb_proj", "L0_ffn_qweights", "L0_ffn_scales", "L0_ffn_biases",
        "L0_ffn_lora_a", "L0_ffn_lora_b", "L0_ffn_ln_gamma", "L0_ffn_ln_beta"]


def kernel(**inputs):
    import numpy as np
    import concourse.bacc as bacc
    from concourse.bass_utils import run_bass_kernel_spmd

    nc = bacc.Bacc("TRN2", target_bir_lowering=False, num_devices=1)
    arrays, args = {}, []
    for name in _INS:
        a = np.ascontiguousarray(inputs[name])
        arrays[f"in_{name}"] = a
        args.append(nc.dram_tensor(f"in_{name}", a.shape, mybir.dt.from_np(a.dtype), kind="ExternalInput").ap())
    out = nc.dram_tensor("out", [1, T, C], F32, kind="ExternalOutput").ap()
    build(nc, *args, out)
    return run_bass_kernel_spmd(nc, [arrays], core_ids=[0]).results[0]["out"]
```
